# Optimizing a Trainium2 kernel written in Bass

```python
import numpy as np
import jax
import jax.numpy as jnp

def _softmax(x, axis=-1):
    return jax.nn.softmax(x, axis=axis)

def _gelu(x):
    return jax.nn.gelu(x, approximate=True)

def _silu(x):
    return jax.nn.silu(x)

def _sigmoid(x):
    return jax.nn.sigmoid(x)

def _layernorm(x, axis=-1, eps=1e-05):
    m = jnp.mean(x, axis=axis, keepdims=True)
    v = jnp.var(x, axis=axis, keepdims=True)
    return (x - m) / jnp.sqrt(v + eps)

def _scatter_add(tgt, idx, src, axis=0):
    return tgt.at[idx].add(src)

def _segment_sum(src, seg, n):
    return jax.ops.segment_sum(src, seg, n)
kernel_name = 'mk_decoder_preln_d1_seqx_r4_38fb36'

def setup_inputs(seed: int=0):
    np.random.seed(seed)
    _w = jnp.asarray

    def _rec_inputs():
        import jax
        import jax.numpy as jnp
        _rk = jax.random.key(seed)
        x = 7.22e-05 + 1 * jax.random.normal(jax.random.fold_in(_rk, 1), (8, 256, 256), jnp.float32)
        _lenS = 256 - jax.random.randint(jax.random.fold_in(_rk, 7), (8,), 0, max(1, 256 // 4) + 1, jnp.int32)
        _lenS2 = 256 - jax.random.randint(jax.random.fold_in(_rk, 8), (8,), 0, max(1, 256 // 4) + 1, jnp.int32)
        _ctx_1024P = jax.random.normal(jax.random.fold_in(_rk, 11), (8, 16, 256), jnp.float32)
        _ctx_1024c = jax.random.dirichlet(jax.random.fold_in(_rk, 511), 0.3 * jnp.ones((16,), jnp.float32), (8, 256))
        _ctx_1024t = jnp.einsum('bsk,bkd->bsd', _ctx_1024c, _ctx_1024P)
        _ctx_1024t = _ctx_1024t * jax.lax.rsqrt(jnp.mean(jnp.square(_ctx_1024t)) + 1e-12) * 0.953939
        ctx_1024 = 4.13588e-05 + 0.999923 * (_ctx_1024t + 0.3 * jax.random.normal(jax.random.fold_in(_rk, 611), (8, 256, 256), jnp.float32))
        return (x, ctx_1024)
    x, ctx_1024 = _rec_inputs()

    def _L0_attn_setup():
        import jax, jax.numpy as jnp
        import numpy as np
        B_, T_, D_ = (8, 1024, 256)

        def _reference_tuple_inner(u, WA, WB, WAf, WBf, w1, w2, b, Wc):
            bsz, seq_len, _ = u.shape
            xf = jnp.concatenate([u[:, :1], jnp.einsum('btd,ed->bte', u[:, 1:], WB)], axis=1)
            xb = jnp.concatenate([jnp.einsum('btd,ed->bte', u[:, 1:], WBf), u[:, -1:]], axis=1)
            gamma = jax.nn.sigmoid(xf @ w1.T + xb @ w2.T + b)
            y = gamma * (xf + xb) + (1.0 - gamma) * u
            final_output = jax.nn.sigmoid(y @ Wc.T).reshape(bsz, seq_len)
            return (y, gamma, final_output)
        key = jax.random.key(seed)
        ks = jax.random.split(key, 9)
        s = 1.0 / np.sqrt(D_)
        return {'u': jax.random.normal(ks[0], (B_, T_, D_), dtype=jnp.float32), 'WA': jax.random.uniform(ks[1], (D_, D_), jnp.float32, -s, s), 'WB': jax.random.uniform(ks[2], (D_, D_), jnp.float32, -s, s), 'WAf': jax.random.uniform(ks[3], (D_, D_), jnp.float32, -s, s), 'WBf': jax.random.uniform(ks[4], (D_, D_), jnp.float32, -s, s), 'w1': jax.random.uniform(ks[5], (1, D_), jnp.float32, -s, s), 'w2': jax.random.uniform(ks[6], (1, D_), jnp.float32, -s, s), 'b': jnp.zeros((1,), dtype=jnp.float32), 'Wc': jax.random.uniform(ks[7], (1, D_), jnp.float32, -s, s)}
    _L0_attn_all = _L0_attn_setup()
    _L0_attn_in = {k: v for k, v in _L0_attn_all.items() if k in ('WA', 'WB', 'WAf', 'WBf', 'w1', 'w2', 'b', 'Wc')}
    del _L0_attn_all

    def _L0_xattn_setup():
        import jax, jax.numpy as jnp
        import numpy as np
        THETA = 10000.0
        SCALE_BASE = 512.0
        GAMMA = 0.96875

        def _dup_interleave(x):
            return jnp.repeat(x, 2, axis=-1)

        def _xpos(x, offset, inverse_scale):
            L, d = (x.shape[-2], x.shape[-1])
            half = d // 2
            base = (jnp.arange(0, d, 2, dtype=x.dtype) + 0.4 * d) / (1.4 * d)
            pos = jnp.arange(offset, offset + L, dtype=x.dtype)
            scale = base[None, :] ** (pos[:, None] / SCALE_BASE)
            freqs = 1.0 / THETA ** (jnp.arange(half, dtype=x.dtype) / half)
            sin_in = pos[:, None] * freqs[None, :]
            if inverse_scale:
                scale = 1.0 / scale
            sin = _dup_interleave(jnp.sin(sin_in) * scale)
            cos = _dup_interleave(jnp.cos(sin_in) * scale)
            rot = jnp.stack((-x[..., 1::2], x[..., ::2]), axis=-1).reshape(x.shape)
            return x * cos + rot * sin

        def _decay_mask(L, gamma, dtype):
            u = jnp.arange(L, dtype=dtype)[:, None]
            v = jnp.arange(L, dtype=dtype)[None, :]
            return jnp.where(u >= v, gamma ** (u - v), jnp.zeros((), dtype))
        key = jax.random.key(seed)
        ks = jax.random.split(key, 6)
        B, L, E = (2, 1024, 256)
        query = jax.random.normal(ks[0], (B, L, E), jnp.float32)
        k_in = jax.random.normal(ks[1], (B, L, E), jnp.float32)
        value = jax.random.normal(ks[2], (B, L, E), jnp.float32)
        s = 1.0 / np.sqrt(E)
        Wq = jax.random.normal(ks[3], (E, E), jnp.float32) * s
        Wk = jax.random.normal(ks[4], (E, E), jnp.float32) * s
        Wv = jax.random.normal(ks[5], (E, E), jnp.float32) * s
        return {'query': query, 'key': k_in, 'value': value, 'Wq': Wq, 'Wk': Wk, 'Wv': Wv}
    _L0_xattn_all = _L0_xattn_setup()
    _L0_xattn_in = {k: v for k, v in _L0_xattn_all.items() if k in ('Wq', 'Wk', 'Wv')}
    del _L0_xattn_all

    def _L0_ffn_setup():
        import jax, jax.numpy as jnp
        import numpy as np
        EPS = 1e-06
        TOP_K = 2

        def rms_norm(x, scale, eps=EPS):
            xf = x.astype(jnp.float32)
            mean_sq = jnp.mean(xf * xf, axis=-1, keepdims=True)
            return (xf * (scale.astype(jnp.float32) * jax.lax.rsqrt(mean_sq + eps))).astype(x.dtype)
        key = jax.random.key(seed)
        k0, k1, k2, k3 = jax.random.split(key, 4)
        B, S, D, H, E = (2, 512, 256, 704, 8)
        x = jax.random.normal(k0, (B, S, D), dtype=jnp.float32)
        norm_scale = jnp.ones((D,), dtype=jnp.float32)
        w_router = jax.random.normal(k1, (E, D), dtype=jnp.float32) * 0.02
        w_up = jax.random.normal(k2, (E, 2 * H, D), dtype=jnp.float32) * 0.02
        w_down = jax.random.normal(k3, (E, D, H), dtype=jnp.float32) * 0.02
        return {'x': x, 'norm_scale': norm_scale, 'w_router': w_router, 'w_up': w_up, 'w_down': w_down}
    _L0_ffn_all = _L0_ffn_setup()
    _L0_ffn_in = {k: v for k, v in _L0_ffn_all.items() if k in ('norm_scale', 'w_router', 'w_up', 'w_down')}
    del _L0_ffn_all
    return {'x': x, 'ctx_1024': ctx_1024, 'L0_attn_WA': _L0_attn_in['WA'], 'L0_attn_WB': _L0_attn_in['WB'], 'L0_attn_WAf': _L0_attn_in['WAf'], 'L0_attn_WBf': _L0_attn_in['WBf'], 'L0_attn_w1': _L0_attn_in['w1'], 'L0_attn_w2': _L0_attn_in['w2'], 'L0_attn_b': _L0_attn_in['b'], 'L0_attn_Wc': _L0_attn_in['Wc'], 'L0_xattn_Wq': _L0_xattn_in['Wq'], 'L0_xattn_Wk': _L0_xattn_in['Wk'], 'L0_xattn_Wv': _L0_xattn_in['Wv'], 'L0_ffn_norm_scale': _L0_ffn_in['norm_scale'], 'L0_ffn_w_router': _L0_ffn_in['w_router'], 'L0_ffn_w_up': _L0_ffn_in['w_up'], 'L0_ffn_w_down': _L0_ffn_in['w_down']}

def reference(x, ctx_1024, L0_attn_WA, L0_attn_WB, L0_attn_WAf, L0_attn_WBf, L0_attn_w1, L0_attn_w2, L0_attn_b, L0_attn_Wc, L0_xattn_Wq, L0_xattn_Wk, L0_xattn_Wv, L0_ffn_norm_scale, L0_ffn_w_router, L0_ffn_w_up, L0_ffn_w_down):
    import jax
    import jax.numpy as jnp

    def _L0_attn_ref(u, WA, WB, WAf, WBf, w1, w2, b, Wc):
        import jax, jax.numpy as jnp
        import numpy as np
        B_, T_, D_ = (8, 1024, 256)

        def _reference_tuple_inner(u, WA, WB, WAf, WBf, w1, w2, b, Wc):
            bsz, seq_len, _ = u.shape
            xf = jnp.concatenate([u[:, :1], jnp.einsum('btd,ed->bte', u[:, 1:], WB)], axis=1)
            xb = jnp.concatenate([jnp.einsum('btd,ed->bte', u[:, 1:], WBf), u[:, -1:]], axis=1)
            gamma = jax.nn.sigmoid(xf @ w1.T + xb @ w2.T + b)
            y = gamma * (xf + xb) + (1.0 - gamma) * u
            final_output = jax.nn.sigmoid(y @ Wc.T).reshape(bsz, seq_len)
            return (y, gamma, final_output)
        return _reference_tuple_inner(u, WA, WB, WAf, WBf, w1, w2, b, Wc)[0]

    def _L0_xattn_ref(query, key, value, Wq, Wk, Wv):
        import jax, jax.numpy as jnp
        import numpy as np
        THETA = 10000.0
        SCALE_BASE = 512.0
        GAMMA = 0.96875

        def _dup_interleave(x):
            return jnp.repeat(x, 2, axis=-1)

        def _xpos(x, offset, inverse_scale):
            L, d = (x.shape[-2], x.shape[-1])
            half = d // 2
            base = (jnp.arange(0, d, 2, dtype=x.dtype) + 0.4 * d) / (1.4 * d)
            pos = jnp.arange(offset, offset + L, dtype=x.dtype)
            scale = base[None, :] ** (pos[:, None] / SCALE_BASE)
            freqs = 1.0 / THETA ** (jnp.arange(half, dtype=x.dtype) / half)
            sin_in = pos[:, None] * freqs[None, :]
            if inverse_scale:
                scale = 1.0 / scale
            sin = _dup_interleave(jnp.sin(sin_in) * scale)
            cos = _dup_interleave(jnp.cos(sin_in) * scale)
            rot = jnp.stack((-x[..., 1::2], x[..., ::2]), axis=-1).reshape(x.shape)
            return x * cos + rot * sin

        def _decay_mask(L, gamma, dtype):
            u = jnp.arange(L, dtype=dtype)[:, None]
            v = jnp.arange(L, dtype=dtype)[None, :]
            return jnp.where(u >= v, gamma ** (u - v), jnp.zeros((), dtype))
        q = jnp.einsum('ble,de->bld', query, Wq)
        k = jnp.einsum('ble,de->bld', key, Wk)
        v = jnp.einsum('ble,de->bld', value, Wv)
        q = _xpos(q, 0, False)
        k = _xpos(k, 0, True)
        L = q.shape[-2]
        mask = _decay_mask(L, jnp.asarray(GAMMA, q.dtype), q.dtype)
        retention = jnp.einsum('bqd,bkd->bqk', q, k) * mask[None, :, :]
        out = jnp.einsum('bqk,bkv->bqv', retention, v)
        return out

    def _L0_ffn_ref(x, norm_scale, w_router, w_up, w_down):
        import jax, jax.numpy as jnp
        import numpy as np
        EPS = 1e-06
        TOP_K = 2

        def rms_norm(x, scale, eps=EPS):
            xf = x.astype(jnp.float32)
            mean_sq = jnp.mean(xf * xf, axis=-1, keepdims=True)
            return (xf * (scale.astype(jnp.float32) * jax.lax.rsqrt(mean_sq + eps))).astype(x.dtype)
        skip = x
        xn = rms_norm(x, norm_scale)
        scores = jnp.einsum('bsd,ed->bse', xn, w_router)
        _, ids = jax.lax.top_k(scores, TOP_K)
        probs = jax.nn.softmax(scores, axis=-1)
        c = jnp.take_along_axis(probs, ids, axis=-1)
        h = jnp.einsum('bsd,ehd->bseh', xn, w_up)
        val, gate = jnp.split(h, 2, axis=-1)
        h = val * jax.nn.silu(gate)
        y = jnp.einsum('bseh,edh->bsed', h, w_down)
        yk = jnp.take_along_axis(y, ids[..., None], axis=2)
        out = jnp.sum(yk * c[..., None], axis=2)
        return out + skip
    x = x + _L0_attn_ref(_layernorm(x, axis=-1), L0_attn_WA, L0_attn_WB, L0_attn_WAf, L0_attn_WBf, L0_attn_w1, L0_attn_w2, L0_attn_b, L0_attn_Wc)
    x = x + _L0_xattn_ref(_layernorm(x, axis=-1), ctx_1024, ctx_1024, L0_xattn_Wq, L0_xattn_Wk, L0_xattn_Wv)
    x = x + _L0_ffn_ref(_layernorm(x, axis=-1), L0_ffn_norm_scale, L0_ffn_w_router, L0_ffn_w_up, L0_ffn_w_down)
    return x

_drawn_inputs = setup_inputs


def setup_inputs(seed=0):
    import zlib

    import numpy as np

    out = dict(_drawn_inputs(seed))
    spreads = {'L0_ffn_norm_scale': (1.0, 0.6)}
    factors = {'L0_ffn_w_router': 8.0, 'L0_ffn_w_up': 8.0, 'L0_ffn_w_down': 8.0}
    for name, (base, spread) in spreads.items():
        noise = np.random.default_rng([zlib.crc32(name.encode()), seed]).standard_normal(out[name].shape)
        drawn = base * np.exp(spread * noise) if base else spread * noise
        out[name] = jnp.asarray(drawn.astype(out[name].dtype))
    for name, factor in factors.items():
        out[name] = (out[name] * factor).astype(out[name].dtype)
    return out
```

```python
import concourse.bass as bass
from concourse import mybir
from contextlib import ExitStack

P = 128
NBATCH = 8
SEQ = 256
D = 256
NT = NBATCH * SEQ // P
NE = 8
H = 704
HC = 352
NH = 6
HLAST = H - (NH - 1) * P
UPC = 2 * 2 * H
DNC = NH * D
NSLOT = 2 * NT + NE - 1
ROWC = D + NE + 1
TAIL = NE + 1
NTOK = NT * P
PADROW = NTOK


def const_layout():
    out = []
    for names in ((("ident", P), ("first", P), ("last", P), ("mask", 384),
                   ("qcos", SEQ), ("qsin", 2 * SEQ), ("kcos", SEQ), ("ksin", 2 * SEQ),
                   ("tokno", NT), ("mhalf", 2), ("eps", 2)),
                  (("before", P), ("ones", P), ("key", NT * NE), ("restart", P), ("steps", P), ("tileno", 40 * NE))):
        at, cols = {}, 0
        for name, n in names:
            at[name] = (cols, cols + n)
            cols += n
        out.append((at, cols))
    return out


def build(nc, x, ctxT, wproj, wproj2, w1, w2, gbias, wq, wk, wv, nscale, wr, wup, wdn, consts, consts2, empty, rows_hbm, out):
    fp32, i32 = mybir.dt.float32, mybir.dt.int32
    ALU, ACT, AX = mybir.AluOpType, mybir.ActivationFunctionType, mybir.AxisListType
    ds = bass.ds
    (at_const, n_const), (at_route, n_route) = const_layout()
    ctx = ExitStack()
    with ctx:
        def sb(name, shape, dt=fp32):
            return ctx.enter_context(nc.sbuf_tensor(name, shape, dt))

        def sem(name):
            return ctx.enter_context(nc.semaphore(name))

        up_w = sb("up_w", [P, NE * UPC])
        dn_w = sb("dn_w", [P, NE * DNC])
        rows = sb("rows", [P, NT, ROWC])
        cst = sb("cst", [P, n_const])
        front = sb("front", [P, 2 * 257 + 3 * 512 + D + 2 * NE + 1])
        small = sb("small", [P, 64 + 4 * NT + 2 * NT + 12 * 4])
        tok_idx = sb("tok_idx", [P, 2 * NT], i32)
        tile_e = sb("tile_e", [1, 40], i32)
        arena = sb("arena", [P, 8104])

        def view(base, lo, *shape):
            n = 1
            for s in shape:
                n *= s
            v = base[:, lo:lo + n]
            if len(shape) == 2:
                v = v.rearrange("p (a b) -> p a b", a=shape[0])
            if len(shape) == 3:
                v = v.rearrange("p (a b c) -> p a b c", a=shape[0], b=shape[1])
            return v

        def const(name):
            lo, hi = at_const[name]
            return cst[:, lo:hi]

        ident, first1, last1 = const("ident"), const("first"), const("last")
        wb_s = view(front, 0, 2, 257)
        wq_s = view(front, 514, 2, D)
        wk_s = view(front, 1026, 2, D)
        wv_s = view(front, 1538, 2, D)
        ns_s = view(front, 2050, D)
        wr_s = view(front, 2050 + D, 2, NE)
        gb_s = view(front, 2050 + D + 2 * NE, 1)
        assert n_route <= 1024
        cst2 = view(front, 514, n_route)

        def route(name):
            lo, hi = at_route[name]
            return cst2[:, lo:hi]

        st6 = view(small, 0, 4, 6)
        mv1 = view(small, 24, 2, 2, 2)
        ve1 = view(small, 32, 2, 2)
        rstd1 = view(small, 36, 2, 2)
        gam = view(small, 40, 2, 2)
        ve2 = view(small, 44, 2, 2)
        mv3 = view(small, 48, 2, 2, 2)
        ve3 = view(small, 56, 2, 2)
        r3 = view(small, 60, 2, 2)
        mv2 = view(small, 64, NT, 2)
        rstd2 = view(small, 64 + 2 * NT, NT)
        base2 = 64 + 3 * NT
        r34 = view(small, base2, 2, 2)
        t34 = view(small, base2 + 4, 2)

        xt = view(arena, 0, 2, 2, D)
        ut = view(arena, 1024, 4, 257)
        xu = view(arena, 2052, 2, 2, D)
        uT = view(arena, 3076, 4, 257)
        dlt = view(arena, 4104, 2, D)
        w1_s = view(arena, 4872, D)
        w2_s = view(arena, 5128, D)
        wbf_s = view(arena, 5384, 2, 257)
        o = 6056
        cT = view(arena, o, 2, 2, SEQ)
        u2 = view(arena, o + 1024, 2, D)
        u2T = view(arena, o + 1536, 2, SEQ)
        rot = view(arena, 0, 2, 2, SEQ)
        kr = view(arena, 1024, 2, 2, SEQ)
        qr = view(arena, 2048, 2, 2, SEQ)
        vt = view(arena, 3072, 2, 2, D)
        retT = view(arena, 4096, 384)
        xn = view(arena, 4480, 2, D)
        sk = view(arena, 4992, 2, D)
        xnT = view(arena, 5504, 2, SEQ)
        assert 5504 + 512 <= o and o + 2048 <= 8104
        sc = sb("sc", [P, NT, NE])
        def rt(n):
            return view(arena, 128 * n, NT, NE)
        dsc, key1, hot1, s2, key2, hot2, both, ex = (rt(n) for n in range(8))
        cntT, cum, excl, pos, pick, d2 = (view(arena, 128 * n, P) for n in range(8, 14))
        vec = 128 * 14
        m1, km1, m2, km2, esum, rsum = (view(arena, vec + NT * n, NT) for n in range(6))
        posf = view(arena, vec + 6 * NT, 2 * NT)
        ntile, ctile, base = (view(arena, vec + 8 * NT + NE * n, NE) for n in range(3))
        tilef = view(arena, vec + 8 * NT + 3 * NE, 40)
        cmpt = view(arena, vec + 8 * NT + 3 * NE + 40, 40 * NE)
        xs = view(arena, 0, 2, ROWC)
        xsT = view(arena, 532, 2, 2 * P)
        sg = view(arena, 1044, 2, HC)
        hh = view(arena, 1748, H)
        hT = view(arena, 2452, NH, P)
        yt = view(arena, 3220, 2, D)
        tail = view(arena, 3732, 2, TAIL)

        bank = [ctx.enter_context(nc.psum_tensor(f"bank{i}", [P, 512], fp32)) for i in range(8)]

        s_cst = sem("constants_loaded")
        s_fw = sem("front_weights_loaded")
        s_upw, s_dnw = sem("up_weights_loaded"), sem("down_weights_loaded")
        s_fill = sem("slots_filled")
        s_pad = sem("pad_rows_zeroed")
        s_empty, s_cst2 = sem("empty_row_loaded"), sem("routing_constants_loaded")
        s_row = sem("rows_complete")
        s_zero = sem("zeros_written")
        s_x = [sem("x_loaded_0"), sem("x_loaded_1")]
        s_col = sem("logit_columns_ready")
        s_st = sem("sums_ready")
        s_mv = sem("mean_var_ready")
        s_ve, s_rstd = sem("var_eps_ready"), sem("rstd_ready")
        s_u, s_uw = sem("u_ready"), sem("edge_logits_ready")
        s_xu = sem("x_plus_u_ready")
        s_tr, s_uT = sem("u_transposed"), sem("uT_ready")
        s_P, s_gam, s_d = sem("projected"), sem("gate_ready"), sem("delta_ready")
        s_x1 = sem("x1_ready")
        s_st2, s_mv2, s_ve2, s_rstd2 = sem("sums2_ready"), sem("mean_var2_ready"), sem("var_eps2_ready"), sem("rstd2_ready")
        s_c = [sem("ctx_loaded_0"), sem("ctx_loaded_1")]
        s_u2, s_tr2, s_u2T = sem("u2_ready"), sem("u2_transposed"), sem("u2T_ready")
        s_K, s_Q, s_V = sem("k_ready"), sem("q_ready"), sem("v_ready")
        s_rk, s_rq = sem("k_bank_read"), sem("q_bank_read")
        s_kr, s_qr = sem("k_rotated"), sem("q_rotated")
        s_vt = sem("v_copied")
        s_R, s_ret = sem("scores_ready"), sem("retention_ready")
        s_O, s_x2 = sem("retained_ready"), sem("x2_ready")
        s_st3, s_mv3, s_ve3, s_r34 = sem("sums3_ready"), sem("mean_var3_ready"), sem("var_eps3_ready"), sem("scales3_ready")
        s_pp = sem("pool_step")
        s_s, s_x2s, s_out0 = sem("skip_ready"), sem("x2_plus_skip_ready"), sem("skip_stored")
        s_xh, s_xn = sem("xhat_ready"), sem("xn_ready")
        s_tr3, s_xnT = sem("xn_transposed"), sem("xnT_ready")
        s_rtr, s_sc = sem("router_ready"), sem("router_scores_copied")
        s_rd = sem("routing_step")
        s_ex = sem("exponents_ready")
        s_cnt = sem("counts_ready")
        s_idx, s_prob, s_te = sem("slots_ready"), sem("probabilities_ready"), sem("tile_experts_ready")
        s_disp = sem("rows_dispatched")
        s_xs = [sem("slot_rows_loaded_0"), sem("slot_rows_loaded_1")]
        s_trx, s_xsT = sem("rows_transposed"), sem("rowsT_ready")
        s_tl = sem("tail_copied")
        s_up = sem("up_part_ready")
        s_sg, s_h = sem("silu_ready"), sem("h_part_ready")
        s_trh, s_hT = sem("h_transposed"), sem("hT_ready")
        s_y, s_yt = sem("y_ready"), sem("y_scaled")
        s_add = sem("y_added")

        spare = sb("spare", [P, 1])

        block = ctx.enter_context(nc.Block())

        def at(it, k, d):
            off = k - d
            return (it * 2 + off if off else it * 2), (it + off // 2 if off // 2 else it), off % 2

        def wait_apart(eng, *waits):
            for s, v in waits:
                eng.wait_ge(s, v)
            nc.vector.tensor_copy(spare[:, :], spare[:, :])

        def live(r, d, n):
            return 0 <= r - d < n

        def steps(eng, step, n, lo, hi):
            for t in range(lo):
                step(t // 2, t % 2, t)
            with eng.Fori(lo // 2, hi // 2) as it:
                step(it, 0, lo)
                step(it, 1, lo + 1)
            for t in range(hi, n):
                step(t // 2, t % 2, t)

        A_STEPS = (NBATCH + 2, 4, 8)
        B_STEPS = (NBATCH + 3, 4, 8)
        E_STEPS = (NSLOT + 2, 4, 38)

        @block.sync
        def _(sp):
            sp.dma_start(cst[:, :], consts).then_inc(s_cst, 16)
            sp.dma_start(rows[:, NT - 1, :], empty).then_inc(s_empty, 16)

            def load_x(it, k, r):
                b, half, slot = at(it, k, 0)
                if r >= 2:
                    sp.wait_ge(s_xu, b - 1)
                sp.dma_start(xt[:, slot], x[ds(b, 1)].rearrange("o (j p) n -> p (o j) n", p=P)).then_inc(s_x[slot], 16)

            load_x(0, 0, 0)
            for dst, src in ((wb_s[:, :, 0:D], wproj), (wbf_s[:, :, 0:D], wproj2), (w1_s, w1.partition_broadcast(P)),
                             (w2_s, w2.partition_broadcast(P)), (gb_s, gbias.partition_broadcast(P))):
                sp.dma_start(dst, src).then_inc(s_fw, 16)
            load_x(0, 1, 1)
            for dst, src in ((wq_s, wq), (wk_s, wk), (wv_s, wv), (ns_s, nscale.partition_broadcast(P)), (wr_s, wr)):
                sp.dma_start(dst, src).then_inc(s_fw, 16)

            def load_ctx(b, slot):
                sp.dma_start(cT[:, slot], ctxT[ds(b, 1)].rearrange("o (c p) n -> p (o c) n", p=P)).then_inc(s_c[slot], 16)

            load_ctx(0, 0)
            load_ctx(1, 1)
            with sp.Fori(1, NBATCH // 2) as it:
                load_x(it, 0, 2)
                load_x(it, 1, 3)

            def step_b(it, k, r):
                if 2 <= r < NBATCH:
                    b, _, slot = at(it, k, 0)
                    sp.wait_ge(s_V, b - 1)
                    load_ctx(b, slot)
                if live(r, 3, NBATCH):
                    b, _, _ = at(it, k, 3)
                    sp.wait_ge(s_x2s, b + 1)
                    sp.dma_start(out[ds(b * SEQ, SEQ), :].rearrange("(j p) n -> p j n", p=P), sk).then_inc(s_out0, 16)

            steps(sp, step_b, *B_STEPS)

            sp.wait_ge(s_Q, NBATCH)
            sp.wait_ge(s_K, NBATCH)
            sp.dma_start(cst2, consts2).then_inc(s_cst2, 16)

            def step_e(it, k, r):
                if live(r, 0, NSLOT):
                    i, _, slot = at(it, k, 0)
                    if r >= 2:
                        sp.wait_ge(s_trx, i - 1)
                        sp.wait_ge(s_tl, i - 1)
                    sp.dma_start(xs[:, slot], rows_hbm[ds(i * P, P), :]).then_inc(s_xs[slot], 16)

            sp.wait_ge(s_disp, 16 * 2 * NT)
            steps(sp, step_e, *E_STEPS)

        @block.scalar
        def _(act):
            act.wait_ge(s_empty, 16)
            act.dma_start(rows_hbm.rearrange("(i p) n -> p i n", p=P),
                          rows[:, NT - 1:NT, :].broadcast_to([P, NSLOT, ROWC])).then_inc(s_fill, 16)
            for e in range(NE):
                act.dma_start(up_w[:, e * UPC:(e + 1) * UPC], wup[e]).then_inc(s_upw, 16)
            for e in range(NE):
                act.dma_start(dn_w[:, e * DNC:(e + 1) * DNC], wdn[e]).then_inc(s_dnw, 16)
            act.wait_ge(s_fw, 160)

            def step_a(it, k, r):
                if live(r, 1, NBATCH):
                    b, _, slot = at(it, k, 1)
                    act.wait_ge(s_tr, b + 1)
                    if r >= 3:
                        act.wait_ge(s_P, b - 1)
                    else:
                        act.wait_ge(s_zero, 1)
                    nc.scalar.activation(uT[:, 2 * slot:2 * slot + 2, 1:SEQ],
                                         bank[slot][:, :].rearrange("p (c n) -> p c n", c=2)[:, :, 1:SEQ],
                                         ACT.Copy).then_inc(s_uT, 1)
                if live(r, 2, NBATCH):
                    b, _, slot = at(it, k, 2)
                    act.wait_ge(s_P, b + 1)
                    for j in range(2):
                        last = nc.scalar.activation(gam[:, slot, j:j + 1], bank[2 + 2 * slot + j][:, D:D + 1],
                                                    ACT.Sigmoid, bias=gb_s)
                    last.then_inc(s_gam, 1)

            steps(act, step_a, *A_STEPS)

            def step_b(it, k, r):
                if live(r, 1, NBATCH):
                    b, _, slot = at(it, k, 1)
                    act.wait_ge(s_V, b + 1)
                    if r >= 3:
                        act.wait_ge(s_O, b - 1)
                    nc.scalar.activation(vt[:, slot], bank[4][:, :].rearrange("p (c n) -> p c n", c=2),
                                         ACT.Copy).then_inc(s_vt, 1)
                if live(r, 0, NBATCH):
                    b, _, _ = at(it, k, 0)
                    act.wait_ge(s_tr2, b + 1)
                    if r >= 1:
                        act.wait_ge(s_Q, b)
                    nc.scalar.activation(u2T, bank[0][:, :].rearrange("p (c n) -> p c n", c=2),
                                         ACT.Copy).then_inc(s_u2T, 1)
                if live(r, 3, NBATCH):
                    b, _, _ = at(it, k, 3)
                    act.wait_ge(s_xn, b + 1)
                    act.wait_ge(s_x2s, b + 1)
                    nc.scalar.activation(rows[:, ds(b * 2, 2), 0:D], xn, ACT.Copy).then_inc(s_row, 1)
                    act.wait_ge(s_tr3, b + 1)
                    if r >= 4:
                        act.wait_ge(s_rtr, b)
                    nc.scalar.activation(xnT, bank[1][:, :].rearrange("p (c n) -> p c n", c=2),
                                         ACT.Copy).then_inc(s_xnT, 1)
                    act.wait_ge(s_rtr, b + 1)
                    nc.scalar.activation(sc[:, ds(b * 2, 2), :],
                                         bank[7][:, 0:2 * NE].rearrange("p (j e) -> p j e", j=2),
                                         ACT.Copy).then_inc(s_sc, 1)

            steps(act, step_b, *B_STEPS)
            act.wait_ge(s_rd, 2)
            nc.scalar.activation(ex, dsc, ACT.Exp).then_inc(s_ex, 1)

            act.wait_ge(s_te, 1)

            def step_e(it, k, r):
                if live(r, 0, NSLOT):
                    i, _, slot = at(it, k, 0)
                    act.wait_ge(s_trx, i + 1)
                    if r >= 2:
                        act.wait_ge(s_up, 4 * i - 4)
                    nc.scalar.activation(xsT[:, slot], bank[4][:, 0:2 * P], ACT.Copy).then_inc(s_xsT, 1)
                if live(r, 1, NSLOT):
                    i, _, _ = at(it, k, 1)
                    for q in range(2):
                        act.wait_ge(s_up, 4 * i + 2 * q + 1)
                        if r >= 2:
                            act.wait_ge(s_h, 2 * i + q - 1)
                        nc.scalar.activation(sg[:, q], bank[2 * q][:, 0:HC], ACT.Silu).then_inc(s_sg, 1)
                if live(r, 2, NSLOT):
                    i, _, slot = at(it, k, 2)
                    e = act.snap(act.value_load(tile_e[0:1, ds(i, 1)], min_val=0, max_val=NE - 1))
                    act.wait_ge(s_y, i + 1)
                    act.wait_ge(s_tl, i + 1)
                    if r >= 4:
                        act.wait_ge(s_add, 16 * i - 16)
                    nc.scalar.activation(yt[:, slot], bank[7][:, 0:D], ACT.Copy,
                                         scale=tail[:, slot, ds(e, 1)]).then_inc(s_yt, 1)

            steps(act, step_e, *E_STEPS)

        @block.gpsimd
        def _(pool):
            pool.memset(uT[:, :, 0:1], 0.0)
            pool.memset(uT[:, :, SEQ:SEQ + 1], 0.0).then_inc(s_zero, 1)
            pool.wait_ge(s_cst, 16)
            pool.wait_ge(s_empty, 16)
            pool.dma_start(out[PADROW:PADROW + P, :], rows[:, NT - 1, 0:D]).then_inc(s_pad, 16)
            mhalf = const("mhalf")

            def step_a(it, k, r):
                if live(r, 0, NBATCH):
                    b, _, slot = at(it, k, 0)
                    pool.wait_ge(s_ve, b + 1)
                    nc.gpsimd.tensor_tensor(rstd1[:, slot], ve1[:, slot], mhalf, ALU.pow).then_inc(s_rstd, 1)
                if live(r, 1, NBATCH):
                    b, _, slot = at(it, k, 1)
                    pool.wait_ge(s_u, b + 1)
                    nc.gpsimd.tensor_tensor(xu[:, slot], xt[:, slot], ut[:, 2 * slot:2 * slot + 2, 0:D],
                                            ALU.add).then_inc(s_xu, 1)
                if live(r, 2, NBATCH):
                    b, _, slot = at(it, k, 2)
                    pool.wait_ge(s_ve2, b + 1)
                    nc.gpsimd.tensor_tensor(rstd2[:, ds(b * 2, 2)], ve2[:, slot], mhalf, ALU.pow).then_inc(s_rstd2, 1)

            steps(pool, step_a, *A_STEPS)

            def step_b(it, k, r):
                if live(r, 1, NBATCH):
                    b, _, slot = at(it, k, 1)
                    for n, (bank_read, rotated, dst) in enumerate(((s_rk, s_kr, kr), (s_rq, s_qr, qr))):
                        pool.wait_ge(bank_read, b + 1)
                        nc.gpsimd.tensor_tensor(dst[:, slot], dst[:, slot], rot[:, n], ALU.add).then_inc(rotated, 1)
                if live(r, 3, NBATCH):
                    b, _, _ = at(it, k, 3)
                    pool.wait_ge(s_s, b + 1)
                    nc.gpsimd.tensor_tensor(sk, sk, rows[:, ds(b * 2, 2), 0:D], ALU.add).then_inc(s_x2s, 1)
                if live(r, 2, NBATCH):
                    b, _, slot = at(it, k, 2)
                    pool.wait_ge(s_ve3, b + 1)
                    nc.gpsimd.tensor_tensor(r3[:, slot], ve3[:, slot], mhalf, ALU.pow).then_inc(s_pp, 1)
                    pool.wait_ge(s_pp, 5 * b + 1)
                    nc.gpsimd.tensor_tensor(t34, r3[:, slot], r3[:, slot], ALU.mult).then_inc(s_pp, 1)
                    pool.wait_ge(s_pp, 5 * b + 2)
                    nc.gpsimd.tensor_tensor(t34, t34, mv3[:, slot, :, 1], ALU.mult).then_inc(s_pp, 1)
                    pool.wait_ge(s_pp, 5 * b + 3)
                    nc.gpsimd.tensor_tensor(t34, t34, const("eps"), ALU.add).then_inc(s_pp, 1)
                    pool.wait_ge(s_pp, 5 * b + 4)
                    nc.gpsimd.tensor_tensor(t34, t34, mhalf, ALU.pow).then_inc(s_pp, 1)
                    pool.wait_ge(s_pp, 5 * b + 5)
                    nc.gpsimd.tensor_tensor(r34[:, slot], t34, r3[:, slot], ALU.mult).then_inc(s_r34, 1)

            steps(pool, step_b, *B_STEPS)

            pool.wait_ge(s_fill, 16)
            pool.wait_ge(s_prob, 1)
            pool.wait_ge(s_row, NBATCH)
            pool.wait_ge(s_idx, 1)
            for n in range(2 * NT):
                pool.indirect_dma_start(out=rows_hbm, out_offset=bass.IndirectOffsetOnAxis(ap=tok_idx[:, n:n + 1], axis=0),
                                        in_=rows[:, n % NT, :], in_offset=None).then_inc(s_disp, 16)
            pool.wait_ge(s_out0, 16 * NBATCH)
            pool.wait_ge(s_pad, 16)

            for i in range(NSLOT):
                pool.wait_ge(s_yt, i + 1)
                if i:
                    pool.wait_ge(s_add, 16 * i)
                pool.indirect_dma_start(out=out, in_=yt[:, i % 2], in_offset=None,
                                        out_offset=bass.IndirectOffsetOnAxis(ap=tail[:, i % 2, NE:NE + 1].bitcast(i32), axis=0),
                                        compute_op=ALU.add).then_inc(s_add, 16)
            pool.wait_ge(s_add, 16 * NSLOT)

        @block.vector
        def _(dve):
            V = nc.vector
            V.memset(spare[:, :], 0.0)
            dve.wait_ge(s_cst, 16)
            dve.wait_ge(s_fw, 160)
            for n, (w, ww) in enumerate(((wb_s, w1_s), (wbf_s, w2_s))):
                for c in range(2):
                    last = V.tensor_tensor_reduce(out=ut[:, 2 * n + c, 0:D], in0=w[:, c, 0:D], in1=ww, scale=1.0, scalar=0.0,
                                                  op0=ALU.mult, op1=ALU.add, accum_out=w[:, c, D:D + 1])
            last.then_inc(s_col, 1)

            def step_a(it, k, r):
                if live(r, 0, NBATCH):
                    b, half, slot = at(it, k, 0)
                    dve.wait_ge(s_x[slot], 16 * half + 16)
                    for j in range(2):
                        last = V.bn_stats(st6[:, j], xt[:, slot, j])
                    last.then_inc(s_st, 1)
                    wait_apart(dve, (s_st, b + 1))
                    for j in range(2):
                        last = V.bn_aggr(mv1[:, slot, j], st6[:, j])
                    last.then_inc(s_mv, 1)
                    dve.wait_ge(s_mv, b + 1)
                    V.tensor_scalar(ve1[:, slot], mv1[:, slot, :, 1], 1e-5, None, ALU.add).then_inc(s_ve, 1)
                if live(r, 1, NBATCH):
                    b, _, slot = at(it, k, 1)
                    dve.wait_ge(s_rstd, b + 1)
                    for j in range(2):
                        last = V.tensor_scalar(ut[:, 2 * slot + j, 0:D], xt[:, slot, j], mv1[:, slot, j, 0:1],
                                               rstd1[:, slot, j:j + 1], ALU.subtract, ALU.mult)
                    last.then_inc(s_u, 1)
                    dve.wait_ge(s_u, b + 1)
                    for j, ww in enumerate((w1_s, w2_s)):
                        last = V.tensor_tensor_reduce(out=bank[6 + j][:, 0:D], in0=ut[:, 2 * slot + j, 0:D], in1=ww, scale=1.0, scalar=0.0,
                                                      op0=ALU.mult, op1=ALU.add, accum_out=ut[:, 2 * slot + j, D:D + 1])
                    last.then_inc(s_uw, 1)
                if live(r, 2, NBATCH):
                    b, _, slot = at(it, k, 2)
                    dve.wait_ge(s_gam, b + 1)
                    for j in range(2):
                        last = V.tensor_tensor(dlt[:, j], bank[2 + 2 * slot + j][:, 0:D], ut[:, 2 * slot + j, 0:D], ALU.subtract)
                    last.then_inc(s_d, 1)
                    dve.wait_ge(s_d, b + 1)
                    dve.wait_ge(s_xu, b + 1)
                    if r == NBATCH + 1:
                        dve.wait_ge(s_fill, 16)
                        dve.wait_ge(s_pad, 16)
                    for j in range(2):
                        last = V.scalar_tensor_tensor(out=rows[:, ds(b * 2 + j, 1), 0:D].squeeze(1), in0=dlt[:, j],
                                                      scalar=gam[:, slot, j:j + 1], in1=xu[:, slot, j],
                                                      op0=ALU.mult, op1=ALU.add)
                    last.then_inc(s_x1, 1)
                    wait_apart(dve, (s_x1, b + 1))
                    for j in range(2):
                        last = V.bn_stats(st6[:, 2 + j], rows[:, ds(b * 2 + j, 1), 0:D].squeeze(1))
                    last.then_inc(s_st2, 1)
                    wait_apart(dve, (s_st2, b + 1))
                    for j in range(2):
                        last = V.bn_aggr(mv3[:, slot, j], st6[:, 2 + j])
                    last.then_inc(s_mv2, 1)
                    dve.wait_ge(s_mv2, b + 1)
                    V.tensor_copy(mv2[:, ds(b * 2, 2), :], mv3[:, slot])
                    V.tensor_scalar(ve2[:, slot], mv3[:, slot, :, 1], 1e-5, None, ALU.add).then_inc(s_ve2, 1)

            steps(dve, step_a, *A_STEPS)
            V.tensor_copy(rows[:, :, ROWC - 1].bitcast(i32), const("tokno"))

            def step_b(it, k, r):
                if live(r, 1, NBATCH):
                    b, _, slot = at(it, k, 1)
                    for n, (ready, rotated, read, used, dst, cos, sin) in enumerate((
                            (s_K, s_kr, s_rk, s_R, kr, const("kcos"), const("ksin")),
                            (s_Q, s_qr, s_rq, s_R, qr, const("qcos"), const("qsin")))):
                        src = bank[2 + n][:, :].rearrange("p (m n) -> p m n", m=2)
                        dve.wait_ge(ready, b + 1)
                        if r >= 2:
                            dve.wait_ge(rotated, b)
                        if r >= 3:
                            dve.wait_ge(used, b - 1)
                        V.tensor_tensor(dst[:, slot], src, cos.unsqueeze(1).broadcast_to([P, 2, SEQ]), ALU.mult)
                        for m in range(2):
                            last = V.tensor_tensor(rot[:, n, m], src[:, 1 - m], sin[:, m * SEQ:(m + 1) * SEQ], ALU.mult)
                        last.then_inc(read, 1)
                if live(r, 3, NBATCH):
                    b, _, slot = at(it, k, 3)
                    dve.wait_ge(s_r34, b + 1)
                    if r >= 4:
                        dve.wait_ge(s_out0, 16 * b)
                    def x2(j):
                        return rows[:, ds(b * 2 + j, 1), 0:D].squeeze(1)

                    for j in range(2):
                        last = V.tensor_scalar(sk[:, j], x2(j), mv3[:, slot, j, 0:1], r3[:, slot, j:j + 1],
                                               ALU.subtract, ALU.mult)
                    last.then_inc(s_s, 1)
                    if r >= 4:
                        dve.wait_ge(s_tr3, b)
                        dve.wait_ge(s_row, b)
                    for j in range(2):
                        last = V.tensor_scalar(xn[:, j], x2(j), mv3[:, slot, j, 0:1], r34[:, slot, j:j + 1],
                                               ALU.subtract, ALU.mult)
                    last.then_inc(s_xh, 1)
                    dve.wait_ge(s_xh, b + 1)
                    V.tensor_tensor(xn, xn, ns_s.unsqueeze(1).broadcast_to([P, 2, D]), ALU.mult).then_inc(s_xn, 1)
                if live(r, 0, NBATCH):
                    b, _, _ = at(it, k, 0)
                    dve.wait_ge(s_rstd2, b + 1)
                    if r >= 1:
                        dve.wait_ge(s_tr2, b)
                    for j in range(2):
                        last = V.tensor_scalar(u2[:, j], rows[:, ds(b * 2 + j, 1), 0:D].squeeze(1),
                                               mv2[:, ds(b * 2 + j, 1), 0], rstd2[:, ds(b * 2 + j, 1)],
                                               ALU.subtract, ALU.mult)
                    last.then_inc(s_u2, 1)
                if live(r, 2, NBATCH):
                    b, _, slot = at(it, k, 2)
                    dve.wait_ge(s_R, b + 1)
                    if r >= 3:
                        dve.wait_ge(s_O, b)
                    V.tensor_tensor(retT, bank[5][:, 0:384], const("mask"), ALU.mult).then_inc(s_ret, 1)
                    dve.wait_ge(s_O, b + 1)
                    V.tensor_tensor(rows[:, ds(b * 2, 2), 0:D], bank[6][:, :].rearrange("p (j n) -> p j n", j=2),
                                    rows[:, ds(b * 2, 2), 0:D], ALU.add).then_inc(s_x2, 1)
                    wait_apart(dve, (s_x2, b + 1))
                    for j in range(2):
                        last = V.bn_stats(st6[:, j], rows[:, ds(b * 2 + j, 1), 0:D].squeeze(1))
                    last.then_inc(s_st3, 1)
                    wait_apart(dve, (s_st3, b + 1))
                    for j in range(2):
                        last = V.bn_aggr(mv3[:, slot, j], st6[:, j])
                    last.then_inc(s_mv3, 1)
                    dve.wait_ge(s_mv3, b + 1)
                    V.tensor_scalar(ve3[:, slot], mv3[:, slot, :, 1], 1e-5, None, ALU.add).then_inc(s_ve3, 1)

            steps(dve, step_b, *B_STEPS)

            done = [0]

            def link(ins):
                done[0] += 1
                ins.then_inc(s_rd, 1)
                dve.wait_ge(s_rd, done[0])

            def wide(v):
                return v.unsqueeze(2).broadcast_to([P, NT, NE])

            key = route("key").rearrange("p (j e) -> p j e", j=NT)
            dve.wait_ge(s_sc, NBATCH)
            dve.wait_ge(s_cst2, 16)
            dve.wait_ge(s_x2s, NBATCH)
            dve.wait_ge(s_out0, 16 * NBATCH)
            link(V.tensor_reduce(m1, sc[:, :, :], AX.X, ALU.max))
            link(V.tensor_tensor(dsc, sc[:, :, :], wide(m1), ALU.subtract))
            link(V.scalar_tensor_tensor(out=key1, in0=dsc, scalar=0.0, in1=key, op0=ALU.is_ge, op1=ALU.mult))
            link(V.tensor_reduce(km1, key1, AX.X, ALU.max))
            link(V.tensor_tensor(hot1, key1, wide(km1), ALU.is_equal))
            link(V.scalar_tensor_tensor(out=s2, in0=hot1, scalar=-1e30, in1=dsc, op0=ALU.mult, op1=ALU.add))
            link(V.tensor_reduce(m2, s2, AX.X, ALU.max))
            link(V.tensor_tensor(key2, s2, wide(m2), ALU.is_equal))
            link(V.tensor_tensor(key2, key2, key, ALU.mult))
            link(V.tensor_reduce(km2, key2, AX.X, ALU.max))
            link(V.tensor_tensor(hot2, key2, wide(km2), ALU.is_equal))
            link(V.tensor_tensor(both, hot1, hot2, ALU.add))
            assert done[0] == 12
            dve.wait_ge(s_ex, 1)
            link(V.tensor_reduce(esum, ex, AX.X, ALU.add))
            link(V.reciprocal(rsum, esum))
            V.tensor_tensor(rows[:, :, D:D + NE], ex, wide(rsum), ALU.mult).then_inc(s_prob, 1)
            dve.wait_ge(s_cnt, 1)
            link(V.tensor_copy(cntT.rearrange("p (e j) -> p e j", e=NE),
                               bank[1][:, 0:P].rearrange("p (j e) -> p e j", j=NT)))
            link(V.tensor_tensor_scan(cum, route("restart"), cntT, 0.0, ALU.mult, ALU.add))
            V.tensor_tensor(excl, cum, cntT, ALU.subtract)
            cum3 = cum.rearrange("p (e j) -> p e j", e=NE)
            link(V.tensor_tensor(pick.rearrange("p (e j) -> p e j", e=NE),
                                 cum3[:, :, NT - 1:NT].broadcast_to([P, NE, NT]),
                                 route("steps").rearrange("p (e j) -> p e j", e=NE), ALU.is_gt))
            link(V.tensor_reduce(ntile, pick.rearrange("p (e j) -> p e j", e=NE), AX.X, ALU.add))
            link(V.tensor_tensor_scan(ctile, route("ones")[:, 0:NE], ntile, 0.0, ALU.mult, ALU.add))
            link(V.tensor_tensor(base, ctile, ntile, ALU.subtract))
            link(V.tensor_scalar(base, base, float(P), None, ALU.mult))
            pos3 = pos.rearrange("p (j e) -> p j e", j=NT)
            link(V.tensor_tensor(pos3, bank[0][:, 0:P].rearrange("p (j e) -> p j e", j=NT),
                                 excl.rearrange("p (e j) -> p j e", e=NE), ALU.add))
            link(V.tensor_tensor(pos3, pos3, base.unsqueeze(1).broadcast_to([P, NT, NE]), ALU.add))
            for n, hot in enumerate((hot1, hot2)):
                link(V.tensor_tensor(pick.rearrange("p (j e) -> p j e", j=NT), hot, pos3, ALU.mult))
                link(V.tensor_reduce(posf[:, n * NT:(n + 1) * NT], pick.rearrange("p (j e) -> p j e", j=NT), AX.X, ALU.add))
            V.tensor_copy(tok_idx[:, :], posf).then_inc(s_idx, 1)
            link(V.tensor_tensor(cmpt[0:1].rearrange("p (i e) -> p i e", e=NE),
                                 ctile[0:1].unsqueeze(1).broadcast_to([1, 40, NE]),
                                 route("tileno")[0:1].rearrange("p (i e) -> p i e", e=NE), ALU.is_le))
            link(V.tensor_reduce(tilef[0:1], cmpt[0:1].rearrange("p (i e) -> p i e", e=NE), AX.X, ALU.add))
            V.tensor_scalar(tile_e[:, :], tilef[0:1], float(NE - 1), None, ALU.min).then_inc(s_te, 1)

            def step_e(it, k, r):
                if live(r, 2, NSLOT):
                    i, _, _ = at(it, k, 2)
                    dve.wait_ge(s_trh, i + 1)
                    if r >= 3:
                        dve.wait_ge(s_y, i)
                    V.tensor_copy(hT[:, 0:4], bank[5][:, :].rearrange("p (c n) -> p c n", c=4))
                    V.tensor_copy(hT[:, 4], bank[6][:, 0:P])
                    V.tensor_copy(hT[0:HLAST, 5], bank[6][0:HLAST, P:2 * P]).then_inc(s_hT, 1)
                if live(r, 1, NSLOT):
                    i, half, slot = at(it, k, 1)
                    dve.wait_ge(s_xs[slot], 16 * half + 16)
                    if r >= 3:
                        dve.wait_ge(s_add, 16 * i - 16)
                    V.tensor_copy(tail[:, slot], xs[:, slot, D:ROWC]).then_inc(s_tl, 1)
                    for q in range(2):
                        dve.wait_ge(s_sg, 2 * i + q + 1)
                        dve.wait_ge(s_up, 4 * i + 2 * q + 2)
                        if r >= 2 and q == 0:
                            dve.wait_ge(s_trh, i)
                        V.tensor_tensor(hh[:, q * HC:(q + 1) * HC], bank[2 * q + 1][:, 0:HC], sg[:, q], ALU.mult).then_inc(s_h, 1)

            steps(dve, step_e, *E_STEPS)

        @block.tensor
        def _(pe):
            T = nc.tensor

            def transposes(dst, src):
                for c in range(2):
                    for j in range(2):
                        last = T.transpose(dst[:, c * SEQ + j * P:c * SEQ + (j + 1) * P], src(j, c), ident)
                return last

            pe.wait_ge(s_cst, 16)

            def step_a(it, k, r):
                if live(r, 1, NBATCH):
                    b, _, slot = at(it, k, 1)
                    pe.wait_ge(s_u, b + 1)
                    if r >= 3:
                        pe.wait_ge(s_uT, b - 1)
                    transposes(bank[slot], lambda j, c: ut[:, 2 * slot + j, c * P:(c + 1) * P]).then_inc(s_tr, 1)
                if live(r, 2, NBATCH):
                    b, _, slot = at(it, k, 2)
                    pe.wait_ge(s_uT, b + 1)
                    pe.wait_ge(s_uw, b + 1)
                    if r == 2:
                        pe.wait_ge(s_col, 1)
                    if r >= 4:
                        pe.wait_ge(s_d, b - 1)
                    for j in range(2):
                        dst = bank[2 + 2 * slot + j][:, 0:257]
                        for c in range(2):
                            T.matmul(dst, uT[:, 2 * slot + c, j * P:(j + 1) * P], wb_s[:, c], start=c == 0, stop=False)
                        for c in range(2):
                            T.matmul(dst, uT[:, 2 * slot + c, j * P + 1:(j + 1) * P + 1], wbf_s[:, c], start=False, stop=False)
                        edge = first1 if j == 0 else last1
                        last = T.matmul(dst, edge, ut[:, 2 * slot + j], start=False, stop=True)
                    last.then_inc(s_P, 1)

            steps(pe, step_a, *A_STEPS)
            pe.wait_ge(s_d, NBATCH)
            pe.wait_ge(s_gam, NBATCH)

            def step_b(it, k, r):
                if live(r, 1, NBATCH):
                    b, half, slot = at(it, k, 1)
                    pe.wait_ge(s_c[slot], 16 * half + 16)
                    if r >= 2:
                        pe.wait_ge(s_rk, b)
                    for m in range(2):
                        for c in range(2):
                            last = T.matmul(bank[2][:, m * SEQ:(m + 1) * SEQ], wk_s[:, c, m * P:(m + 1) * P], cT[:, slot, c],
                                            start=c == 0, stop=c == 1)
                    last.then_inc(s_K, 1)
                    pe.wait_ge(s_u2T, b + 1)
                    if r >= 2:
                        pe.wait_ge(s_rq, b)
                    for m in range(2):
                        for c in range(2):
                            last = T.matmul(bank[3][:, m * SEQ:(m + 1) * SEQ], wq_s[:, c, m * P:(m + 1) * P], u2T[:, c],
                                            start=c == 0, stop=c == 1)
                    last.then_inc(s_Q, 1)
                    if r >= 2:
                        pe.wait_ge(s_vt, b)
                    for j in range(2):
                        for c in range(2):
                            last = T.matmul(bank[4][:, j * D:(j + 1) * D], cT[:, slot, c, j * P:(j + 1) * P], wv_s[:, c],
                                            start=c == 0, stop=c == 1)
                    last.then_inc(s_V, 1)
                if live(r, 2, NBATCH):
                    b, _, slot = at(it, k, 2)
                    pe.wait_ge(s_kr, b + 1)
                    pe.wait_ge(s_qr, b + 1)
                    if r >= 3:
                        pe.wait_ge(s_ret, b)
                    for m in range(2):
                        T.matmul(bank[5][:, 0:SEQ], kr[:, slot, m, 0:P], qr[:, slot, m, :], start=m == 0, stop=m == 1)
                    for m in range(2):
                        last = T.matmul(bank[5][:, SEQ:SEQ + P], kr[:, slot, m, P:SEQ], qr[:, slot, m, P:SEQ],
                                        start=m == 0, stop=m == 1)
                    last.then_inc(s_R, 1)
                if live(r, 0, NBATCH):
                    b, _, _ = at(it, k, 0)
                    pe.wait_ge(s_u2, b + 1)
                    if r >= 1:
                        pe.wait_ge(s_u2T, b)
                    transposes(bank[0], lambda j, c: u2[:, j, c * P:(c + 1) * P]).then_inc(s_tr2, 1)
                if live(r, 3, NBATCH):
                    b, _, _ = at(it, k, 3)
                    pe.wait_ge(s_xn, b + 1)
                    if r >= 4:
                        pe.wait_ge(s_xnT, b)
                    transposes(bank[1], lambda j, c: xn[:, j, c * P:(c + 1) * P]).then_inc(s_tr3, 1)
                if live(r, 2, NBATCH):
                    b, _, slot = at(it, k, 2)
                    pe.wait_ge(s_ret, b + 1)
                    pe.wait_ge(s_vt, b + 1)
                    if r >= 3:
                        pe.wait_ge(s_x2, b)
                    T.matmul(bank[6][:, 0:D], retT[:, 0:P], vt[:, slot, 0], start=True, stop=True)
                    T.matmul(bank[6][:, D:2 * D], retT[:, P:SEQ], vt[:, slot, 0], start=True, stop=False)
                    T.matmul(bank[6][:, D:2 * D], retT[:, SEQ:SEQ + P], vt[:, slot, 1], start=False, stop=True).then_inc(s_O, 1)
                if live(r, 3, NBATCH):
                    b, _, _ = at(it, k, 3)
                    pe.wait_ge(s_xnT, b + 1)
                    if r >= 4:
                        pe.wait_ge(s_sc, b)
                    for j in range(2):
                        for c in range(2):
                            last = T.matmul(bank[7][:, j * NE:(j + 1) * NE], xnT[:, c, j * P:(j + 1) * P], wr_s[:, c],
                                            start=c == 0, stop=c == 1)
                    last.then_inc(s_rtr, 1)

            steps(pe, step_b, *B_STEPS)

            pe.wait_ge(s_rd, 12)
            both2 = both.rearrange("p j e -> p (j e)")
            T.matmul(bank[0][:, 0:P], route("before"), both2, start=True, stop=True)
            T.matmul(bank[1][:, 0:P], route("ones"), both2, start=True, stop=True).then_inc(s_cnt, 1)

            pe.wait_ge(s_upw, 16 * NE)
            pe.wait_ge(s_dnw, 16 * NE)
            pe.wait_ge(s_te, 1)

            def step_e(it, k, r):
                if live(r, 2, NSLOT):
                    i, _, _ = at(it, k, 2)
                    pe.wait_ge(s_h, 2 * i + 2)
                    if r >= 3:
                        pe.wait_ge(s_hT, i)
                    for c in range(NH):
                        w = P if c < NH - 1 else HLAST
                        dst = bank[5 + c // 4]
                        last = T.transpose(dst[0:w, (c % 4) * P:(c % 4 + 1) * P], hh[:, c * P:c * P + w], ident)
                    last.then_inc(s_trh, 1)
                if live(r, 0, NSLOT):
                    i, half, slot = at(it, k, 0)
                    pe.wait_ge(s_xs[slot], 16 * half + 16)
                    if r >= 1:
                        pe.wait_ge(s_xsT, i)
                    for c in range(2):
                        last = T.transpose(bank[4][:, c * P:(c + 1) * P], xs[:, slot, c * P:(c + 1) * P], ident)
                    last.then_inc(s_trx, 1)
                if live(r, 1, NSLOT):
                    i, _, slot = at(it, k, 1)
                    w0 = pe.snap(pe.value_load(tile_e[0:1, ds(i, 1)], min_val=0, max_val=NE - 1) * UPC)
                    pe.wait_ge(s_xsT, i + 1)
                    for q in range(4):
                        if r >= 2 and q % 2 == 0:
                            pe.wait_ge(s_h, 2 * i + q // 2 - 1)
                        for c in range(2):
                            n0 = c * 2 * H + (1 - q % 2) * H + (q // 2) * HC
                            last = T.matmul(bank[q][:, 0:HC], xsT[:, slot, c * P:(c + 1) * P], up_w[:, ds(w0 + n0, HC)],
                                            start=c == 0, stop=c == 1)
                        last.then_inc(s_up, 1)
                if live(r, 2, NSLOT):
                    i, _, _ = at(it, k, 2)
                    w0 = pe.snap(pe.value_load(tile_e[0:1, ds(i, 1)], min_val=0, max_val=NE - 1) * DNC)
                    pe.wait_ge(s_hT, i + 1)
                    if r >= 3:
                        pe.wait_ge(s_yt, i)
                    for c in range(NH):
                        w = P if c < NH - 1 else HLAST
                        last = T.matmul(bank[7][:, 0:D], hT[0:w, c], dn_w[0:w, ds(w0 + c * D, D)], start=c == 0, stop=c == NH - 1)
                    last.then_inc(s_y, 1)

            steps(pe, step_e, *E_STEPS)


def constants():
    import numpy as np
    (at1, n1), (at2, n2) = const_layout()
    a, b = np.zeros((P, n1), np.float32), np.zeros((P, n2), np.float32)

    def put(arr, at, name, v):
        lo, hi = at[name]
        arr[:, lo:hi] = v

    p = np.arange(P)
    put(a, at1, "ident", np.eye(P))
    put(a, at1, "first", (p[:, None] == 0) & (p[None] == 0))
    put(a, at1, "last", (p[:, None] == P - 1) & (p[None] == P - 1))
    u = np.arange(SEQ, dtype=np.float32)
    block = lambda u, v: np.where(u >= v, np.float32(0.96875) ** np.maximum(u - v, 0), 0)
    put(a, at1, "mask", np.concatenate([block(u[None], u[:P, None]), block(u[None, P:], u[P:, None])], 1))
    base = (np.arange(0, D, 2, dtype=np.float32) + np.float32(0.4 * D)) / np.float32(1.4 * D)
    scale = base[:, None] ** (u[None] / np.float32(512.0))
    freq = np.float32(1.0) / np.float32(10000.0) ** (np.arange(P, dtype=np.float32) / np.float32(P))
    angle = freq[:, None] * u[None]
    for n, s in (("q", scale), ("k", 1 / scale)):
        put(a, at1, n + "cos", np.cos(angle) * s)
        put(a, at1, n + "sin", np.concatenate([-np.sin(angle) * s, np.sin(angle) * s], 1))
    put(a, at1, "tokno", np.arange(NT)[None] * P + p[:, None])
    put(a, at1, "mhalf", -0.5)
    put(a, at1, "eps", 1e-6)
    put(b, at2, "before", p[:, None] < p[None])
    put(b, at2, "ones", 1.0)
    put(b, at2, "key", np.tile(NE - np.arange(NE), NT)[None])
    put(b, at2, "restart", (np.arange(P) % NT != 0)[None])
    put(b, at2, "steps", np.tile(np.arange(NT) * P, NE)[None])
    put(b, at2, "tileno", np.repeat(np.arange(40), NE)[None])
    empty = np.zeros((P, ROWC), np.float32)
    empty[:, ROWC - 1] = (PADROW + p).astype(np.int32).view(np.float32)
    return a, b, empty


def kernel(**inputs):
    import numpy as np
    import concourse.bacc as bacc
    from concourse import mybir as mb
    from concourse.bass_utils import run_bass_kernel_spmd as run

    v = {k: np.asarray(a) for k, a in inputs.items()}

    def chunks(w):
        return np.ascontiguousarray(w.reshape(2, P, -1).transpose(1, 0, 2))

    def evens_first(w):
        return w.reshape(D, P, 2).transpose(0, 2, 1).reshape(D, D)

    w_down = np.zeros((NE, NH * P, D), np.float32)
    w_down[:, :H] = v["L0_ffn_w_down"].transpose(0, 2, 1)
    cst, cst2, empty = constants()
    arrays = {
        "x": v["x"],
        "ctxT": np.ascontiguousarray(v["ctx_1024"].transpose(0, 2, 1)),
        "wproj": chunks(v["L0_attn_WB"].T),
        "wproj2": chunks(v["L0_attn_WBf"].T),
        "w1": v["L0_attn_w1"].reshape(D),
        "w2": v["L0_attn_w2"].reshape(D),
        "gbias": v["L0_attn_b"].reshape(1),
        "wq": chunks(evens_first(v["L0_xattn_Wq"].T)),
        "wk": chunks(evens_first(v["L0_xattn_Wk"].T)),
        "wv": chunks(v["L0_xattn_Wv"].T),
        "nscale": v["L0_ffn_norm_scale"].reshape(D),
        "wr": chunks(v["L0_ffn_w_router"].T),
        "wup": np.ascontiguousarray(v["L0_ffn_w_up"].transpose(0, 2, 1).reshape(NE, 2, P, 2 * H)
                                    .transpose(0, 2, 1, 3).reshape(NE, P, UPC)),
        "wdn": np.ascontiguousarray(w_down.reshape(NE, NH, P, D).transpose(0, 2, 1, 3).reshape(NE, P, DNC)),
        "consts": cst,
        "consts2": cst2,
        "empty": empty,
    }
    nc = bacc.Bacc("TRN2", target_bir_lowering=False, num_devices=1)
    args = [nc.dram_tensor(f"in_{n}", a.shape, mb.dt.float32, kind="ExternalInput").ap() for n, a in arrays.items()]
    rows_hbm = nc.dram_tensor("slot_rows", (NSLOT * P, ROWC), mb.dt.float32, kind="Internal").ap()
    out = nc.dram_tensor("out", (NTOK + P, D), mb.dt.float32, kind="ExternalOutput").ap()
    build(nc, *args, rows_hbm, out)
    r = run(nc, [{f"in_{n}": np.asarray(a, np.float32) for n, a in arrays.items()}], core_ids=[0])
    return r.results[0]["out"][:NTOK].reshape(NBATCH, SEQ, D)
```

```python
import concourse.bass as bass
from concourse import mybir
from contextlib import ExitStack

P = 128
NBATCH = 8
SEQ = 256
D = 256
NT = NBATCH * SEQ // P
NE = 8
H = 704
HC = 352
NH = 6
HLAST = H - (NH - 1) * P
UPC = 2 * 2 * H
DNC = NH * D
NSLOT = 2 * NT + NE - 1
W1 = D + 2
NTOK = NT * P
PADROW = NTOK
XROW = D + NE
XSCALE = 1024.0
WSCALE = 16384.0


def const_layout():
    out = []
    for names in ((("ident", P), ("first", P), ("last", P), ("ones", P), ("mhalf", NT), ("eps", 2), ("minus", NT)),
                  (("mask", 384), ("qcos", SEQ), ("qsin", 2 * SEQ), ("kcos", SEQ), ("ksin", 2 * SEQ)),
                  (("before", P), ("key", NT * NE), ("restart", P), ("steps", P), ("tileno", 40 * NE),
                   ("column", P), ("tokno", 2 * NT), ("padrow", 1))):
        at, cols = {}, 0
        for name, n in names:
            at[name] = (cols, cols + n)
            cols += n
        out.append((at, cols))
    return out


def build(nc, x, ctxT, wproj, wproj2, w1, w2, gbias, wq, wk, wv, nscale, wr, wup, wdn, consts, consts_b, consts2, xrow_hbm, out):
    fp32, fp16, bf16, i32 = mybir.dt.float32, mybir.dt.float16, mybir.dt.bfloat16, mybir.dt.int32
    ALU, ACT, AX = mybir.AluOpType, mybir.ActivationFunctionType, mybir.AxisListType
    ds = bass.ds
    (at_const, n_const), (at_const_b, n_const_b), (at_route, n_route) = const_layout()
    ctx = ExitStack()
    with ctx:
        def sb(name, shape, dt=fp32):
            return ctx.enter_context(nc.sbuf_tensor(name, shape, dt))

        def sem(name):
            return ctx.enter_context(nc.semaphore(name))

        expert_w = sb("expert_w", [P, NE * (UPC + DNC)])
        up_raw = expert_w[:, UPC:(NE + 1) * UPC]
        up_w = expert_w[:, 0:NE * UPC].bitcast(fp16)
        dn_w = expert_w[:, NE * UPC:NE * (UPC + DNC)]
        assert UPC <= 2 * DNC
        rows = sb("rows", [P, NT, D])
        cst = sb("cst", [P, n_const])
        cst_b = sb("cst_b", [P, n_const_b])
        front = sb("front", [P, 2 * W1 + 3 * 512 + 2 + 2 * NE + 1])
        ident16 = sb("ident16", [P, P], fp16)
        small = sb("small", [P, 64 + 4 * NT + 22 + 64])
        take_idx = sb("take_idx", [P, NSLOT], i32)
        add_idx = sb("add_idx", [P, NSLOT], i32)
        tile_e = sb("tile_e", [1, 40], i32)
        arena = sb("arena", [P, 8104])

        def view(base, lo, *shape):
            n = 1
            for s in shape:
                n *= s
            v = base[:, lo:lo + n]
            if len(shape) == 2:
                v = v.rearrange("p (a b) -> p a b", a=shape[0])
            if len(shape) == 3:
                v = v.rearrange("p (a b c) -> p a b c", a=shape[0], b=shape[1])
            return v

        def const(name):
            if name in at_const:
                lo, hi = at_const[name]
                return cst[:, lo:hi]
            lo, hi = at_const_b[name]
            return cst_b[:, lo:hi]

        ident, first1, last1 = const("ident"), const("first"), const("last")
        wb_s = view(front, 0, 2, W1)
        o = 2 * W1
        wq_s = view(front, o, 2, D)
        wk_s = view(front, o + 512, 2, D)
        wv_s = view(front, o + 1024, 2, D)
        ns_s = view(front, o + 1536, 2)
        wr_s = view(front, o + 1538, 2, NE)
        gb_s = view(front, o + 1538 + 2 * NE, 1)
        assert n_route <= 1536
        cst2 = view(front, o, n_route)

        def route(name):
            lo, hi = at_route[name]
            return cst2[:, lo:hi]

        st6 = view(small, 0, 4, 6)
        mv1 = view(small, 24, 2, 2, 2)
        ve1 = view(small, 32, 2, 2)
        rstd1 = view(small, 36, 2, 2)
        gam = view(small, 40, 2, 2)
        mv3 = view(small, 48, 2, 2, 2)
        ve3 = view(small, 56, 2, 2)
        r3 = view(small, 60, 2, 2)
        rstd2 = view(small, 64, NT)
        nb2 = view(small, 64 + NT, NT)
        o = 64 + 2 * NT
        r4 = view(small, o, 2, 2)
        t4 = view(small, o + 4, 2)
        nb1 = view(small, o + 6, 2, 2)
        nb3 = view(small, o + 10, 2, 2)
        mv2 = view(small, o + 14, 2, 2)
        ve2, mean2 = view(small, o + 18, NT), view(small, o + 18 + NT, NT)
        o += 18 + 2 * NT + 4
        sq = view(small, o, 2 * NE)
        fro = view(small, o + 2 * NE, NE)
        inv_fro = view(small, o + 3 * NE, NE)
        up_scale = view(small, o + 4 * NE, 2 * NE)
        descale = view(small, o + 6 * NE, NE)

        ut = view(arena, 0, 4, W1)
        xu = view(arena, 1032, 2, 2, D)
        uT = view(arena, 2056, 4, W1)
        dlt = view(arena, 3088, 2, D)
        w1_s = view(arena, 3600, D)
        w2_s = view(arena, 3856, D)
        wbf_s = view(arena, 4112, 2, W1)
        squares = view(arena, 4112 + 2 * W1, 2 * H // 2).bitcast(bf16)
        o = 6056
        cT = view(arena, o, 2, 2, SEQ)
        u2 = view(arena, o + 1024, 2, D)
        u2T = view(arena, o + 1536, 2, SEQ)
        rot = view(arena, 0, 2, 2, SEQ)
        kr = view(arena, 1024, 2, 2, SEQ)
        qr = view(arena, 2048, 2, 2, SEQ)
        vt = view(arena, 3072, 2, 2, D)
        retT = view(arena, 4096, 384)
        xn = view(arena, 4480, 2, D)
        sk = view(arena, 4992, 2, D)
        xnT = view(arena, 5504, 2, SEQ)
        xrow_f = sb("xrow", [P, 2 * D])
        xrow = xrow_f[:, :].bitcast(fp16).rearrange("p (j n) -> p j n", j=2)
        assert 5504 + 512 <= o and 4112 + 2 * W1 + H <= o and o + 2048 <= 8104
        sc = sb("sc", [P, NT, NE])
        def rt(n):
            return view(arena, 128 * n, NT, NE)
        dsc, key1, hot1, s2, key2, hot2, both, ex = (rt(n) for n in range(8))
        cntT, cum, excl, pos, pick, d2 = (view(arena, 128 * n, P) for n in range(8, 14))
        vec = 128 * 14
        m1, km1, m2, km2, esum, rsum = (view(arena, vec + NT * n, NT) for n in range(6))
        posf = view(arena, vec + 8 * NT, 2 * NT)
        posi = view(arena, vec + 10 * NT, 2, 2 * NT).bitcast(i32)
        slotf = view(arena, vec + 14 * NT, 2, 2 * NT)
        o = vec + 18 * NT
        ntile, ctile, base = (view(arena, o + NE * n, NE) for n in range(3))
        tilef = view(arena, o + 3 * NE, 40)
        cmpt = view(arena, o + 3 * NE + 40, 40 * NE)
        o += 3 * NE + 40 + 40 * NE
        in_tile = view(arena, o, NT * NSLOT).bitcast(fp16).rearrange("p (a n) -> p a n", n=NSLOT)
        o += NT * NSLOT
        marks = view(arena, o, NT * NSLOT).bitcast(fp16).rearrange("p (a n) -> p a n", n=NSLOT)
        o += NT * NSLOT
        in_col = view(arena, o, NT * P).bitcast(fp16).rearrange("p (a n) -> p a n", n=P)
        empty = view(arena, 0, NSLOT)
        assert o + NT * P <= 8104
        xs_row = view(arena, 0, 2, XROW)
        xs = view(arena, 0, 2 * XROW).bitcast(fp16).rearrange("p (s n) -> p s n", s=2)
        xsT = view(arena, 1120, 2 * 2 * P).bitcast(fp16).rearrange("p (s n) -> p s n", s=2)
        pair_scale = view(arena, 1104, 2)
        gate_scale = view(arena, 1108, 2)
        sg = view(arena, 1728, 2, HC)
        hh = view(arena, 2432, H)
        hT = view(arena, 3136, NH, P)
        yt = view(arena, 3904, 2, D)

        bank = [ctx.enter_context(nc.psum_tensor(f"bank{i}", [P, 512], fp32)) for i in range(8)]

        s_cst = sem("constants_loaded")
        s_fw = sem("front_weights_loaded")
        s_fwb, s_cstb = sem("stage_b_weights_loaded"), sem("stage_b_constants_loaded")
        s_upw, s_dnw = [sem("up_weights_loaded_0"), sem("up_weights_loaded_1")], sem("down_weights_loaded")
        s_sq, s_fro, s_scl = sem("squares_summed"), sem("norm_ready"), sem("weight_scale_step")
        s_hi, s_lo = sem("weights_high_ready"), sem("weights_low_ready")
        s_wr = sem("router_weights_scaled")
        s_pad = sem("pad_rows_zeroed")
        s_cst2 = sem("routing_constants_loaded")
        s_row = sem("xn_stored")
        s_nb1, s_nb2, s_pa = sem("bias1_ready"), sem("bias2_ready"), sem("pool_step_a")
        s_zero = sem("zeros_written")
        s_x = [sem(f"x_loaded_{b}") for b in range(NBATCH)]
        s_col = sem("logit_columns_ready")
        s_st = sem("sums_ready")
        s_mv = sem("mean_var_ready")
        s_ve, s_rstd = sem("var_eps_ready"), sem("rstd_ready")
        s_u, s_uw = sem("u_ready"), sem("edge_logits_ready")
        s_xu = sem("x_plus_u_ready")
        s_tr, s_uT = sem("u_transposed"), sem("uT_ready")
        s_P, s_gam, s_d = sem("projected"), sem("gate_ready"), sem("delta_ready")
        s_x1 = sem("x1_ready")
        s_st2, s_mv2, s_ve2, s_rstd2 = sem("sums2_ready"), sem("mean_var2_ready"), sem("var_eps2_ready"), sem("rstd2_ready")
        s_c = [sem("ctx_loaded_0"), sem("ctx_loaded_1")]
        s_u2, s_tr2, s_u2T = sem("u2_ready"), sem("u2_transposed"), sem("u2T_ready")
        s_K, s_Q, s_V = sem("k_ready"), sem("q_ready"), sem("v_ready")
        s_rk, s_rq = sem("k_bank_read"), sem("q_bank_read")
        s_kr, s_qr = sem("k_rotated"), sem("q_rotated")
        s_vt = sem("v_copied")
        s_R, s_ret = sem("scores_ready"), sem("retention_ready")
        s_O, s_x2 = sem("retained_ready"), sem("x2_ready")
        s_st3, s_mv3, s_ve3, s_r34 = sem("sums3_ready"), sem("mean_var3_ready"), sem("var_eps3_ready"), sem("scales3_ready")
        s_pp = sem("pool_step")
        s_s, s_x2s, s_out0 = sem("skip_ready"), sem("x2_plus_skip_ready"), sem("skip_stored")
        s_xh, s_xl, s_xn = sem("xn_high_ready"), sem("xn_low_ready"), sem("xn_ready")
        s_tr3, s_xnT = sem("xn_transposed"), sem("xnT_ready")
        s_rtr, s_sc = sem("router_ready"), sem("router_scores_copied")
        s_rd = sem("routing_step")
        s_ex = sem("exponents_ready")
        s_cnt = sem("counts_ready")
        s_prob, s_te = sem("probabilities_ready"), sem("tile_experts_ready")
        s_probs, s_ps = sem("probabilities_stored"), sem("pair_scale_ready")
        s_gs = sem("gate_scale_ready")
        s_mark, s_col32, s_tab = sem("pair_marks_ready"), sem("pair_columns_ready"), sem("slot_table_summed")
        s_take = sem("slot_table_ready")
        s_xs = [sem("slot_rows_loaded_0"), sem("slot_rows_loaded_1")]
        s_trx, s_xsT = sem("rows_transposed"), sem("rowsT_ready")
        s_up = sem("up_part_ready")
        s_sg, s_h = sem("silu_ready"), sem("h_part_ready")
        s_trh, s_hT = sem("h_transposed"), sem("hT_ready")
        s_y, s_yt = sem("y_ready"), sem("y_scaled")
        s_add = sem("y_added")

        spare = sb("spare", [P, 2])
        pad_zero = sb("pad_zero", [P, D])

        rowsT_bank = bank[4][:, 0:2 * P].bitcast(fp16)

        block = ctx.enter_context(nc.Block())

        def at(it, k, d):
            off = k - d
            return (it * 2 + off if off else it * 2), (it + off // 2 if off // 2 else it), off % 2

        def wait_apart(eng, *waits):
            for s, v in waits:
                eng.wait_ge(s, v)
            nc.vector.tensor_copy(spare[:, 0:1], spare[:, 0:1])

        def live(r, d, n):
            return 0 <= r - d < n

        def steps(eng, step, n, lo, hi):
            for t in range(lo):
                step(t // 2, t % 2, t)
            with eng.Fori(lo // 2, hi // 2) as it:
                step(it, 0, lo)
                step(it, 1, lo + 1)
            for t in range(hi, n):
                step(t // 2, t % 2, t)

        def raw_chunk(e, c):
            return up_raw[:, ds(e * UPC + c * 2 * H, 2 * H)]

        def part(e, c, low):
            return up_w[:, ds(e * 2 * UPC + c * UPC + low * 2 * H, 2 * H)]

        def split_chunks(it, k, r):
            if r < 2:
                return [(2 * r + n // 2, n % 2) for n in range(4)]
            if r < 4:
                return [(r + 2, 0), (r + 2, 1)]
            return [(it + 4, k)] if r < NBATCH else []

        A_STEPS = (NBATCH + 3, 4, 8)
        B_STEPS = (NBATCH + 4, 4, 8)
        E_STEPS = (NSLOT + 2, 4, 38)

        @block.sync
        def _(sp):
            def load_x(b):
                sp.dma_start(rows[:, 2 * b:2 * b + 2, :], x[b].rearrange("(j p) n -> p j n", p=P)).then_inc(s_x[b], 16)

            load_x(0)
            sp.dma_start(cst[:, :], consts).then_inc(s_cst, 16)
            load_x(1)
            for dst, src in ((w1_s, w1.partition_broadcast(P)), (w2_s, w2.partition_broadcast(P)), (wb_s[:, :, 0:D], wproj),
                             (wbf_s[:, :, 0:D], wproj2), (gb_s, gbias.partition_broadcast(P)), (ns_s, nscale)):
                sp.dma_start(dst, src).then_inc(s_fw, 16)
            for b in range(2, NBATCH):
                load_x(b)

            def load_ctx(b, slot):
                sp.dma_start(cT[:, slot], ctxT[ds(b, 1)].rearrange("o (c p) n -> p (o c) n", p=P)).then_inc(s_c[slot], 16)

            load_ctx(0, 0)
            load_ctx(1, 1)
            for dst, src in ((wk_s, wk), (wq_s, wq), (wv_s, wv), (wr_s, wr)):
                sp.dma_start(dst, src).then_inc(s_fwb, 16)
            sp.dma_start(cst_b[:, :], consts_b).then_inc(s_cstb, 16)
            def load_up(e, k):
                sp.dma_start(up_raw[:, ds(e * UPC, UPC)], wup[ds(e, 1)].rearrange("o p n -> (o p) n")).then_inc(s_upw[k], 16)

            load_up(0, 0)
            load_up(1, 1)
            with sp.Fori(1, NE // 2) as it:
                for k in range(2):
                    sp.wait_ge(s_sq, 4 * it + 2 * k - 2)
                    load_up(it * 2 + k if k else it * 2, k)

            def step_b(it, k, r):
                if 2 <= r < NBATCH:
                    b, _, slot = at(it, k, 0)
                    sp.wait_ge(s_V, b - 1)
                    load_ctx(b, slot)
                if 2 <= r < NE:
                    e, _, _ = at(it, k, 0)
                    load_down(e)
                if r == NBATCH:
                    sp.wait_ge(s_V, NBATCH)
                    sp.dma_start(cst2, consts2).then_inc(s_cst2, 16)
                if live(r, 3, NBATCH):
                    b, _, _ = at(it, k, 3)
                    sp.wait_ge(s_xl, b + 1)
                    sp.dma_start(xrow_hbm[ds(b * SEQ, SEQ), 0:D].rearrange("(j p) n -> p j n", p=P),
                                 xrow_f[:, :].rearrange("p (j n) -> p j n", j=2)).then_inc(s_row, 16)
                    sp.wait_ge(s_x2s, b + 1)
                    sp.dma_start(out[ds(b * SEQ, SEQ), :].rearrange("(j p) n -> p j n", p=P), rows[:, ds(b * 2, 2), :]).then_inc(s_out0, 16)

            def load_down(e):
                sp.dma_start(dn_w[:, ds(e * DNC, DNC)], wdn[ds(e, 1)].rearrange("o p n -> (o p) n")).then_inc(s_dnw, 16)

            steps(sp, step_b, *B_STEPS)
            for e in range(2):
                sp.wait_ge(s_lo, 2 * NE)
                load_down(e)
            sp.wait_ge(s_prob, 1)
            sp.dma_start(xrow_hbm[:, D:XROW].rearrange("(j p) n -> p j n", p=P), ex).then_inc(s_probs, 16)

        @block.scalar
        def _(act):
            act.wait_ge(s_cst, 16)
            act.wait_ge(s_fw, 96)
            nc.scalar.activation(ident16[:, :], ident, ACT.Copy).then_inc(s_sc, 1)

            def step_a(it, k, r):
                if live(r, 1, NBATCH):
                    b, _, slot = at(it, k, 1)
                    act.wait_ge(s_nb1, b + 1)
                    if r >= 3:
                        act.wait_ge(s_d, b - 1)
                        act.wait_ge(s_P, b - 1)
                    for j in range(2):
                        last = nc.scalar.activation(ut[:, 2 * slot + j, 0:D], rows[:, ds(b * 2 + j, 1), :].squeeze(1), ACT.Identity,
                                                    bias=nb1[:, slot, j:j + 1], scale=rstd1[:, slot, j:j + 1])
                    last.then_inc(s_u, 1)
                if live(r, 2, NBATCH):
                    b, _, slot = at(it, k, 2)
                    act.wait_ge(s_P, b + 1)
                    for j in range(2):
                        last = nc.scalar.activation(gam[:, slot, j:j + 1], bank[2 + 2 * slot + j][:, D:D + 1],
                                                    ACT.Sigmoid, bias=gb_s)
                    last.then_inc(s_gam, 1)
                if live(r, 1, NBATCH):
                    b, _, slot = at(it, k, 1)
                    act.wait_ge(s_tr, b + 1)
                    if r >= 3:
                        act.wait_ge(s_P, b - 1)
                    else:
                        act.wait_ge(s_zero, 1)
                    nc.scalar.activation(uT[:, 2 * slot:2 * slot + 2, 1:SEQ],
                                         bank[slot][:, :].rearrange("p (c n) -> p c n", c=2)[:, :, 1:SEQ],
                                         ACT.Copy).then_inc(s_uT, 1)
                if live(r, 2, NE):
                    e, half, slot = at(it, k, 2)
                    act.wait_ge(s_upw[slot], 16 * half + 16)
                    for c in range(2):
                        if r > 2 or c:
                            act.wait_ge(s_sq, 2 * e + c)
                        nc.scalar.activation(squares, raw_chunk(e, c), ACT.Square, scale=ns_s[:, c:c + 1],
                                             accum_out=sq[:, ds(e * 2 + c, 1)]).then_inc(s_sq, 1)

            steps(act, step_a, *A_STEPS)

            def high_parts(it, k, r):
                for n, (e, c) in enumerate(split_chunks(it, k, r)):
                    if r == 0 and n == 0:
                        act.wait_ge(s_scl, 4)
                    if r or n > 1:
                        act.wait_ge(s_lo, e * 2 + c - 1)
                    nc.scalar.activation(part(e, c, 0), raw_chunk(e, c), ACT.Copy,
                                         scale=up_scale[:, ds(e * 2 + c, 1)]).then_inc(s_hi, 1)

            def step_b(it, k, r):
                if r >= 2:
                    high_parts(it, k, r)
                if live(r, 3, NBATCH):
                    b, _, slot = at(it, k, 3)
                    act.wait_ge(s_r34, b + 1)
                    if r >= 4:
                        act.wait_ge(s_x2s, b)
                    for j in range(2):
                        last = nc.scalar.activation(sk[:, j], rows[:, ds(b * 2 + j, 1), :].squeeze(1), ACT.Identity,
                                                    bias=nb3[:, slot, j:j + 1], scale=r3[:, slot, j:j + 1])
                    last.then_inc(s_s, 1)
                if live(r, 0, NBATCH):
                    b, _, _ = at(it, k, 0)
                    act.wait_ge(s_nb2, b + 1)
                    if r >= 1:
                        act.wait_ge(s_tr2, b)
                    for j in range(2):
                        last = nc.scalar.activation(u2[:, j], rows[:, ds(b * 2 + j, 1), :].squeeze(1), ACT.Identity,
                                                    bias=nb2[:, ds(b * 2 + j, 1)], scale=rstd2[:, ds(b * 2 + j, 1)])
                    last.then_inc(s_u2, 1)
                if live(r, 1, NBATCH):
                    b, _, slot = at(it, k, 1)
                    act.wait_ge(s_V, b + 1)
                    if r == 1:
                        act.wait_ge(s_x1, NBATCH)
                    if r >= 3:
                        act.wait_ge(s_O, b - 1)
                    nc.scalar.activation(vt[:, slot], bank[4][:, :].rearrange("p (c n) -> p c n", c=2),
                                         ACT.Copy).then_inc(s_vt, 1)
                if live(r, 0, NBATCH):
                    b, _, _ = at(it, k, 0)
                    act.wait_ge(s_tr2, b + 1)
                    if r >= 1:
                        act.wait_ge(s_Q, b)
                    nc.scalar.activation(u2T, bank[0][:, :].rearrange("p (c n) -> p c n", c=2),
                                         ACT.Copy).then_inc(s_u2T, 1)
                if live(r, 3, NBATCH):
                    b, _, _ = at(it, k, 3)
                    act.wait_ge(s_tr3, b + 1)
                    if r >= 4:
                        act.wait_ge(s_rtr, b)
                    nc.scalar.activation(xnT, bank[1][:, :].rearrange("p (c n) -> p c n", c=2),
                                         ACT.Copy).then_inc(s_xnT, 1)
                    if r >= 4:
                        act.wait_ge(s_row, 16 * b)
                    nc.scalar.activation(xrow[:, :, 0:D], xn, ACT.Copy).then_inc(s_xh, 1)
                if r < 2:
                    high_parts(it, k, r)
                if live(r, 4, NBATCH):
                    b, _, _ = at(it, k, 4)
                    act.wait_ge(s_rtr, b + 1)
                    nc.scalar.activation(sc[:, ds(b * 2, 2), :],
                                         bank[7][:, 0:2 * NE].rearrange("p (j e) -> p j e", j=2),
                                         ACT.Copy).then_inc(s_sc, 1)

            steps(act, step_b, *B_STEPS)
            act.wait_ge(s_rd, 2)
            nc.scalar.activation(ex, dsc, ACT.Exp).then_inc(s_ex, 1)
            nc.scalar.activation(spare[:, 1:2], const("mhalf")[:, 0:1], ACT.Silu)

            act.wait_ge(s_take, 1)
            act.wait_ge(s_scl, 6)

            def step_e(it, k, r):
                if live(r, 0, NSLOT):
                    i, _, slot = at(it, k, 0)
                    act.wait_ge(s_trx, i + 1)
                    if r >= 2:
                        act.wait_ge(s_up, 4 * i - 4)
                    nc.scalar.activation(xsT[:, slot], rowsT_bank, ACT.Copy).then_inc(s_xsT, 1)
                if live(r, 1, NSLOT):
                    i, _, slot = at(it, k, 1)
                    e = act.snap(act.value_load(tile_e[0:1, ds(i, 1)], min_val=0, max_val=NE - 1))
                    nc.scalar.activation(gate_scale[:, slot:slot + 1], descale[:, ds(e, 1)], ACT.Copy).then_inc(s_gs, 1)
                    act.wait_ge(s_gs, i + 1)
                    for q in range(2):
                        act.wait_ge(s_up, 4 * i + 2 * q + 1)
                        if r >= 2:
                            act.wait_ge(s_h, 2 * i + q - 1)
                        nc.scalar.activation(sg[:, q], bank[2 * q][:, 0:HC], ACT.Silu,
                                             scale=gate_scale[:, slot:slot + 1]).then_inc(s_sg, 1)
                if live(r, 2, NSLOT):
                    i, _, slot = at(it, k, 2)
                    act.wait_ge(s_y, i + 1)
                    if r >= 4:
                        act.wait_ge(s_add, 16 * i - 16)
                    nc.scalar.activation(yt[:, slot], bank[7][:, 0:D], ACT.Copy).then_inc(s_yt, 1)

            steps(act, step_e, *E_STEPS)

        @block.gpsimd
        def _(pool):
            pool.memset(uT[:, :, 0:1], 0.0)
            pool.memset(uT[:, :, SEQ:SEQ + 1], 0.0).then_inc(s_zero, 1)
            pool.memset(pad_zero[:, :], 0.0).then_inc(s_zero, 1)
            pool.wait_ge(s_zero, 2)
            pool.dma_start(out[PADROW:PADROW + P, :], pad_zero[:, :]).then_inc(s_pad, 16)
            pool.wait_ge(s_cst, 16)
            mhalf, minus, eps = const("mhalf"), const("minus"), const("eps")

            def step_a(it, k, r):
                if live(r, 0, NBATCH):
                    b, _, slot = at(it, k, 0)
                    pool.wait_ge(s_ve, b + 1)
                    nc.gpsimd.tensor_tensor(rstd1[:, slot], ve1[:, slot], mhalf[:, 0:2], ALU.pow).then_inc(s_rstd, 1)
                    pool.wait_ge(s_rstd, 2 * b + 1)
                    nc.gpsimd.tensor_tensor(nb1[:, slot], mv1[:, slot, :, 0], rstd1[:, slot], ALU.mult).then_inc(s_rstd, 1)
                    pool.wait_ge(s_rstd, 2 * b + 2)
                    if r >= 1:
                        pool.wait_ge(s_u, b)
                    if r >= 3:
                        pool.wait_ge(s_x1, b - 2)
                    nc.gpsimd.tensor_tensor(nb1[:, slot], nb1[:, slot], minus[:, 0:2], ALU.mult).then_inc(s_nb1, 1)
                if live(r, 1, NBATCH):
                    b, _, slot = at(it, k, 1)
                    if r == NBATCH:
                        pool.wait_ge(s_u, NBATCH)
                        pool.wait_ge(s_x1, NBATCH - 2)
                    nc.gpsimd.tensor_tensor(xu[:, slot], rows[:, ds(b * 2, 2), :], ut[:, 2 * slot:2 * slot + 2, 0:D],
                                            ALU.add).then_inc(s_xu, 1)
                if r >= NBATCH:
                    m, lo, hi = r - NBATCH, (0, NT - 4, NT - 2)[r - NBATCH], (NT - 4, NT - 2, NT)[r - NBATCH]
                    pool.wait_ge(s_ve2, hi // 2)
                    nc.gpsimd.tensor_tensor(rstd2[:, lo:hi], ve2[:, lo:hi], mhalf[:, 0:hi - lo], ALU.pow).then_inc(s_rstd2, 1)
                    pool.wait_ge(s_rstd2, 2 * m + 1)
                    nc.gpsimd.tensor_tensor(nb2[:, lo:hi], mean2[:, lo:hi], rstd2[:, lo:hi], ALU.mult).then_inc(s_rstd2, 1)
                    pool.wait_ge(s_rstd2, 2 * m + 2)
                    nc.gpsimd.tensor_tensor(nb2[:, lo:hi], nb2[:, lo:hi], minus[:, 0:hi - lo], ALU.mult).then_inc(s_nb2, (hi - lo) // 2)

            steps(pool, step_a, *A_STEPS)
            pool.wait_ge(s_scl, 2)
            nc.gpsimd.tensor_tensor(inv_fro, fro, mhalf[:, 0:NE], ALU.pow).then_inc(s_scl, 1)

            def step_b(it, k, r):
                if live(r, 1, NBATCH):
                    b, _, slot = at(it, k, 1)
                    for n, (bank_read, rotated, dst) in enumerate(((s_rk, s_kr, kr), (s_rq, s_qr, qr))):
                        pool.wait_ge(bank_read, b + 1)
                        if n and r >= 3:
                            pool.wait_ge(s_xn, b - 1)
                        nc.gpsimd.tensor_tensor(dst[:, slot], dst[:, slot], rot[:, n], ALU.add).then_inc(rotated, 1)
                if live(r, 3, NBATCH):
                    b, _, _ = at(it, k, 3)
                    if r > NBATCH:
                        pool.wait_ge(s_xn, r - 2)
                    nc.gpsimd.tensor_tensor(rows[:, ds(b * 2, 2), :], sk, rows[:, ds(b * 2, 2), :], ALU.add).then_inc(s_x2s, 1)
                    pool.wait_ge(s_xh, b + 1)
                    nc.gpsimd.tensor_tensor(xrow[:, :, D:2 * D], xn, xrow[:, :, 0:D], ALU.subtract).then_inc(s_xl, 1)
                if live(r, 2, NBATCH):
                    b, _, slot = at(it, k, 2)
                    pool.wait_ge(s_ve3, b + 1)
                    for n, (dst, a, c, op) in enumerate((
                            (r3[:, slot], ve3[:, slot], mhalf[:, 0:2], ALU.pow),
                            (t4, r3[:, slot], r3[:, slot], ALU.mult),
                            (nb3[:, slot], mv3[:, slot, :, 0], r3[:, slot], ALU.mult),
                            (t4, t4, mv3[:, slot, :, 1], ALU.mult),
                            (nb3[:, slot], nb3[:, slot], minus[:, 0:2], ALU.mult),
                            (t4, t4, eps, ALU.add))):
                        if n:
                            pool.wait_ge(s_pp, 6 * b + n)
                        nc.gpsimd.tensor_tensor(dst, a, c, op).then_inc(s_pp, 1)
                    pool.wait_ge(s_pp, 6 * b + 6)
                    nc.gpsimd.tensor_tensor(r4[:, slot], t4, mhalf[:, 0:2], ALU.pow).then_inc(s_r34, 1)
            steps(pool, step_b, *B_STEPS)

            pool.wait_ge(s_out0, 16 * NBATCH)
            pool.wait_ge(s_pad, 16)
            pool.wait_ge(s_row, 16 * NBATCH)
            pool.wait_ge(s_probs, 16)
            pool.wait_ge(s_take, 1)

            def take(i):
                if i >= 2:
                    pool.wait_ge(s_trx, i - 1)
                    pool.wait_ge(s_ps, i - 1)
                pool.indirect_dma_start(out=xs_row[:, i % 2], out_offset=None, in_=xrow_hbm,
                                        in_offset=bass.IndirectOffsetOnAxis(ap=take_idx[:, i:i + 1], axis=0)).then_inc(s_xs[i % 2], 16)

            for i in range(3):
                take(i)
            for i in range(NSLOT):
                if i + 3 < NSLOT:
                    take(i + 3)
                pool.wait_ge(s_yt, i + 1)
                if i:
                    pool.wait_ge(s_add, 16 * i)
                pool.indirect_dma_start(out=out, in_=yt[:, i % 2], in_offset=None,
                                        out_offset=bass.IndirectOffsetOnAxis(ap=add_idx[:, i:i + 1], axis=0),
                                        compute_op=ALU.add).then_inc(s_add, 16)
            pool.wait_ge(s_add, 16 * NSLOT)

        @block.vector
        def _(dve):
            V = nc.vector
            V.memset(spare[:, 0:1], 0.0)
            dve.wait_ge(s_cst, 16)
            V.memset(wb_s[:, :, D + 1], 0.0)
            V.memset(wbf_s[:, :, D + 1], 0.0)
            V.memset(ut[:, :, D + 1], 0.0)
            def step_a(it, k, r):
                if live(r, 3, NBATCH):
                    b, _, slot = at(it, k, 3)
                    dve.wait_ge(s_gam, b + 1)
                    for j in range(2):
                        last = V.tensor_tensor(dlt[:, j], bank[2 + 2 * slot + j][:, 0:D], ut[:, 2 * slot + j, 0:D], ALU.subtract)
                    last.then_inc(s_d, 1)
                    dve.wait_ge(s_d, b + 1)
                    dve.wait_ge(s_xu, b + 1)
                    for j in range(2):
                        last = V.scalar_tensor_tensor(out=rows[:, ds(b * 2 + j, 1), :].squeeze(1), in0=dlt[:, j],
                                                      scalar=gam[:, slot, j:j + 1], in1=xu[:, slot, j],
                                                      op0=ALU.mult, op1=ALU.add)
                    last.then_inc(s_x1, 1)
                    wait_apart(dve, (s_x1, b + 1))
                    for j in range(2):
                        last = V.bn_stats(st6[:, 2 + j], rows[:, ds(b * 2 + j, 1), :].squeeze(1))
                    last.then_inc(s_st2, 1)
                    wait_apart(dve, (s_st2, b + 1))
                    for j in range(2):
                        last = V.bn_aggr(mv2[:, j], st6[:, 2 + j])
                    last.then_inc(s_mv2, 1)
                    dve.wait_ge(s_mv2, b + 1)
                    V.tensor_scalar(mean2[:, ds(b * 2, 2)], mv2[:, :, 0], 0.0, None, ALU.add)
                    V.tensor_scalar(ve2[:, ds(b * 2, 2)], mv2[:, :, 1], 1e-5, None, ALU.add).then_inc(s_ve2, 1)
                if live(r, 0, NBATCH):
                    b, _, slot = at(it, k, 0)
                    if r < 4 or r >= NBATCH:
                        dve.wait_ge(s_x[r], 16)
                    elif r == 4:
                        for later in range(4, NBATCH):
                            dve.wait_ge(s_x[later], 16)
                    for j in range(2):
                        last = V.bn_stats(st6[:, j], rows[:, ds(b * 2 + j, 1), :].squeeze(1))
                    last.then_inc(s_st, 1)
                    wait_apart(dve, (s_st, b + 1))
                    for j in range(2):
                        last = V.bn_aggr(mv1[:, slot, j], st6[:, j])
                    last.then_inc(s_mv, 1)
                    dve.wait_ge(s_mv, b + 1)
                    V.tensor_scalar(ve1[:, slot], mv1[:, slot, :, 1], 1e-5, None, ALU.add).then_inc(s_ve, 1)
                if r == 0:
                    dve.wait_ge(s_fw, 96)
                    for n, (w, ww) in enumerate(((wb_s, w1_s), (wbf_s, w2_s))):
                        for c in range(2):
                            last = V.tensor_tensor_reduce(out=bank[6 + n][:, c * D:(c + 1) * D], in0=w[:, c, 0:D], in1=ww,
                                                          scale=1.0, scalar=0.0, op0=ALU.mult, op1=ALU.add, accum_out=w[:, c, D:D + 1])
                    last.then_inc(s_col, 1)
                if live(r, 1, NBATCH):
                    b, _, slot = at(it, k, 1)
                    dve.wait_ge(s_u, b + 1)
                    for j, ww in enumerate((w1_s, w2_s)):
                        last = V.tensor_tensor_reduce(out=bank[6 + j][:, 0:D], in0=ut[:, 2 * slot + j, 0:D], in1=ww, scale=1.0, scalar=0.0,
                                                      op0=ALU.mult, op1=ALU.add, accum_out=ut[:, 2 * slot + j, D:D + 1])
                    last.then_inc(s_uw, 1)

            steps(dve, step_a, *A_STEPS)

            dve.wait_ge(s_fro, 1)
            V.tensor_reduce(fro, bank[5][:, 0:2 * NE].rearrange("p (e c) -> p e c", c=2), AX.X, ALU.add).then_inc(s_scl, 1)
            dve.wait_ge(s_scl, 1)
            V.tensor_scalar(fro, fro, 1e-30, None, ALU.max).then_inc(s_scl, 1)
            dve.wait_ge(s_fwb, 64)
            for c in range(2):
                V.tensor_scalar(wr_s[:, c], wr_s[:, c], ns_s[:, c:c + 1], 1.0 / XSCALE, ALU.mult, ALU.mult).then_inc(s_wr, 1)
            dve.wait_ge(s_scl, 3)
            for c in range(2):
                last = V.tensor_scalar(up_scale.rearrange("p (e c) -> p e c", c=2)[:, :, c], inv_fro, ns_s[:, c:c + 1], WSCALE,
                                       ALU.mult, ALU.mult)
            last.then_inc(s_scl, 1)
            V.tensor_scalar(descale, inv_fro, WSCALE * XSCALE, None, ALU.mult).then_inc(s_scl, 1)
            dve.wait_ge(s_scl, 5)
            V.reciprocal(descale, descale).then_inc(s_scl, 1)
            dve.wait_ge(s_cstb, 16)

            def low_parts(it, k, r):
                for e, c in split_chunks(it, k, r):
                    dve.wait_ge(s_hi, e * 2 + c + 1)
                    V.scalar_tensor_tensor(out=part(e, c, 1), in0=raw_chunk(e, c), scalar=up_scale[:, ds(e * 2 + c, 1)],
                                           in1=part(e, c, 0), op0=ALU.mult, op1=ALU.subtract).then_inc(s_lo, 1)

            def step_b(it, k, r):
                if live(r, 2, NBATCH):
                    b, _, slot = at(it, k, 2)
                    dve.wait_ge(s_R, b + 1)
                    if r >= 3:
                        dve.wait_ge(s_O, b)
                    V.tensor_tensor(retT, bank[5][:, 0:384], const("mask"), ALU.mult).then_inc(s_ret, 1)
                if live(r, 1, NBATCH):
                    b, _, slot = at(it, k, 1)
                    for n, (ready, rotated, read, used, dst, cos, sin) in enumerate((
                            (s_K, s_kr, s_rk, s_R, kr, const("kcos"), const("ksin")),
                            (s_Q, s_qr, s_rq, s_R, qr, const("qcos"), const("qsin")))):
                        src = bank[2 + n][:, :].rearrange("p (m n) -> p m n", m=2)
                        dve.wait_ge(ready, b + 1)
                        if r >= 2:
                            dve.wait_ge(rotated, b)
                        if r >= 3:
                            dve.wait_ge(used, b - 1)
                        V.tensor_tensor(dst[:, slot], src, cos.unsqueeze(1).broadcast_to([P, 2, SEQ]), ALU.mult)
                        for m in range(2):
                            last = V.tensor_tensor(rot[:, n, m], src[:, 1 - m], sin[:, m * SEQ:(m + 1) * SEQ], ALU.mult)
                        last.then_inc(read, 1)
                if live(r, 3, NBATCH):
                    b, _, slot = at(it, k, 3)
                    dve.wait_ge(s_s, b + 1)
                    if r >= 4:
                        dve.wait_ge(s_tr3, b)
                        dve.wait_ge(s_xl, b)
                    for j in range(2):
                        last = V.tensor_scalar(xn[:, j], sk[:, j], r4[:, slot, j:j + 1], XSCALE, ALU.mult, ALU.mult)
                    last.then_inc(s_xn, 1)
                low_parts(it, k, r)
                if live(r, 2, NBATCH):
                    b, _, slot = at(it, k, 2)
                    dve.wait_ge(s_O, b + 1)
                    V.tensor_tensor(rows[:, ds(b * 2, 2), :], bank[6][:, :].rearrange("p (j n) -> p j n", j=2),
                                    rows[:, ds(b * 2, 2), :], ALU.add).then_inc(s_x2, 1)
                    wait_apart(dve, (s_x2, b + 1))
                    for j in range(2):
                        last = V.bn_stats(st6[:, 2 + j], rows[:, ds(b * 2 + j, 1), :].squeeze(1))
                    last.then_inc(s_st3, 1)
                    wait_apart(dve, (s_st3, b + 1))
                    for j in range(2):
                        last = V.bn_aggr(mv3[:, slot, j], st6[:, 2 + j])
                    last.then_inc(s_mv3, 1)
                    dve.wait_ge(s_mv3, b + 1)
                    V.tensor_scalar(ve3[:, slot], mv3[:, slot, :, 1], 1e-5, None, ALU.add).then_inc(s_ve3, 1)

            steps(dve, step_b, *B_STEPS)

            done = [0]

            def link(ins):
                done[0] += 1
                ins.then_inc(s_rd, 1)
                dve.wait_ge(s_rd, done[0])

            def wide(v):
                return v.unsqueeze(2).broadcast_to([P, NT, NE])

            key = route("key").rearrange("p (j e) -> p j e", j=NT)
            dve.wait_ge(s_sc, NBATCH + 1)
            dve.wait_ge(s_cst2, 16)
            dve.wait_ge(s_O, NBATCH)
            link(V.tensor_reduce(m1, sc[:, :, :], AX.X, ALU.max))
            link(V.tensor_tensor(dsc, sc[:, :, :], wide(m1), ALU.subtract))
            link(V.scalar_tensor_tensor(out=key1, in0=dsc, scalar=0.0, in1=key, op0=ALU.is_ge, op1=ALU.mult))
            link(V.tensor_reduce(km1, key1, AX.X, ALU.max))
            link(V.tensor_tensor(hot1, key1, wide(km1), ALU.is_equal))
            link(V.scalar_tensor_tensor(out=s2, in0=hot1, scalar=-1e30, in1=dsc, op0=ALU.mult, op1=ALU.add))
            link(V.tensor_reduce(m2, s2, AX.X, ALU.max))
            link(V.tensor_tensor(key2, s2, wide(m2), ALU.is_equal))
            link(V.tensor_tensor(key2, key2, key, ALU.mult))
            link(V.tensor_reduce(km2, key2, AX.X, ALU.max))
            link(V.tensor_tensor(hot2, key2, wide(km2), ALU.is_equal))
            link(V.tensor_tensor(both, hot1, hot2, ALU.add))
            assert done[0] == 12
            dve.wait_ge(s_ex, 1)
            link(V.tensor_reduce(esum, ex, AX.X, ALU.add))
            link(V.reciprocal(rsum, esum))
            V.tensor_tensor(ex, ex, wide(rsum), ALU.mult).then_inc(s_prob, 1)
            dve.wait_ge(s_cnt, 1)
            link(V.tensor_copy(cntT.rearrange("p (e j) -> p e j", e=NE),
                               bank[1][:, 0:P].rearrange("p (j e) -> p e j", j=NT)))
            link(V.tensor_tensor_scan(cum, route("restart"), cntT, 0.0, ALU.mult, ALU.add))
            V.tensor_tensor(excl, cum, cntT, ALU.subtract)
            cum3 = cum.rearrange("p (e j) -> p e j", e=NE)
            link(V.tensor_tensor(pick.rearrange("p (e j) -> p e j", e=NE),
                                 cum3[:, :, NT - 1:NT].broadcast_to([P, NE, NT]),
                                 route("steps").rearrange("p (e j) -> p e j", e=NE), ALU.is_gt))
            link(V.tensor_reduce(ntile, pick.rearrange("p (e j) -> p e j", e=NE), AX.X, ALU.add))
            link(V.tensor_tensor_scan(ctile, const("ones")[:, 0:NE], ntile, 0.0, ALU.mult, ALU.add))
            link(V.tensor_tensor(base, ctile, ntile, ALU.subtract))
            link(V.tensor_scalar(base, base, float(P), None, ALU.mult))
            pos3 = pos.rearrange("p (j e) -> p j e", j=NT)
            link(V.tensor_tensor(pos3, bank[0][:, 0:P].rearrange("p (j e) -> p j e", j=NT),
                                 excl.rearrange("p (e j) -> p j e", e=NE), ALU.add))
            link(V.tensor_tensor(pos3, pos3, base.unsqueeze(1).broadcast_to([P, NT, NE]), ALU.add))
            for n, hot in enumerate((hot1, hot2)):
                link(V.tensor_tensor(pick.rearrange("p (j e) -> p j e", j=NT), hot, pos3, ALU.mult))
                link(V.tensor_reduce(posf[:, n * NT:(n + 1) * NT], pick.rearrange("p (j e) -> p j e", j=NT), AX.X, ALU.add))
            link(V.tensor_copy(posi[:, 1], posf))
            link(V.tensor_scalar(posi[:, 0], posi[:, 1], P - 1, None, ALU.bitwise_and))
            link(V.tensor_scalar(posi[:, 1], posi[:, 1], 7, None, ALU.arith_shift_right))
            link(V.tensor_copy(slotf, posi))
            link(V.tensor_tensor(in_tile, slotf[:, 1].unsqueeze(2).broadcast_to([P, 2 * NT, NSLOT]),
                                 route("column")[:, 0:NSLOT].unsqueeze(1).broadcast_to([P, 2 * NT, NSLOT]), ALU.is_equal))
            V.tensor_tensor(marks, in_tile, route("tokno").unsqueeze(2).broadcast_to([P, 2 * NT, NSLOT]),
                            ALU.mult).then_inc(s_mark, 1)
            dve.wait_ge(s_xl, NBATCH)
            dve.wait_ge(s_rtr, NBATCH)
            for n in range(4):
                part_n = slice(8 * n, 8 * n + 8)
                V.tensor_tensor(in_col[:, part_n], slotf[:, 0, part_n].unsqueeze(2).broadcast_to([P, 8, P]),
                                route("column").unsqueeze(1).broadcast_to([P, 8, P]), ALU.is_equal).then_inc(s_col32, 1)
            link(V.tensor_tensor(cmpt[0:1].rearrange("p (i e) -> p i e", e=NE),
                                 ctile[0:1].unsqueeze(1).broadcast_to([1, 40, NE]),
                                 route("tileno")[0:1].rearrange("p (i e) -> p i e", e=NE), ALU.is_le))
            link(V.tensor_reduce(tilef[0:1], cmpt[0:1].rearrange("p (i e) -> p i e", e=NE), AX.X, ALU.add))
            V.tensor_scalar(tile_e[:, :], tilef[0:1], float(NE - 1), None, ALU.min).then_inc(s_te, 1)

            table = bank[2][:, 0:NSLOT]
            dve.wait_ge(s_tab, 1)
            V.tensor_scalar(take_idx[:, :], table, -1.0, 0.0, ALU.add, ALU.max)
            link(V.tensor_scalar(empty, table, 0.0, route("padrow"), ALU.is_equal, ALU.mult))
            V.scalar_tensor_tensor(out=add_idx[:, :], in0=table, scalar=-1.0, in1=empty,
                                   op0=ALU.add, op1=ALU.add).then_inc(s_take, 1)

            def step_e(it, k, r):
                if live(r, 2, NSLOT):
                    i, _, _ = at(it, k, 2)
                    dve.wait_ge(s_trh, i + 1)
                    if r >= 3:
                        dve.wait_ge(s_y, i)
                    V.tensor_copy(hT[:, 0:4], bank[5][:, :].rearrange("p (c n) -> p c n", c=4))
                    V.tensor_copy(hT[:, 4], bank[6][:, 0:P])
                    V.tensor_copy(hT[0:HLAST, 5], bank[6][0:HLAST, P:2 * P]).then_inc(s_hT, 1)
                if live(r, 1, NSLOT):
                    i, half, slot = at(it, k, 1)
                    e = dve.snap(dve.value_load(tile_e[0:1, ds(i, 1)], min_val=0, max_val=NE - 1))
                    dve.wait_ge(s_xs[slot], 16 * half + 16)
                    V.tensor_tensor(pair_scale[:, slot:slot + 1], xs_row[:, slot, ds(e + D, 1)], descale[:, ds(e, 1)],
                                    ALU.mult).then_inc(s_ps, 1)
                    dve.wait_ge(s_ps, i + 1)
                    for q in range(2):
                        dve.wait_ge(s_sg, 2 * i + q + 1)
                        dve.wait_ge(s_up, 4 * i + 2 * q + 2)
                        if r >= 2 and q == 0:
                            dve.wait_ge(s_trh, i)
                        V.scalar_tensor_tensor(out=hh[:, q * HC:(q + 1) * HC], in0=bank[2 * q + 1][:, 0:HC],
                                               scalar=pair_scale[:, slot:slot + 1], in1=sg[:, q],
                                               op0=ALU.mult, op1=ALU.mult).then_inc(s_h, 1)

            steps(dve, step_e, *E_STEPS)

        @block.tensor
        def _(pe):
            T = nc.tensor

            def transposes(dst, src):
                for c in range(2):
                    for j in range(2):
                        last = T.transpose(dst[:, c * SEQ + j * P:c * SEQ + (j + 1) * P], src(j, c), ident)
                return last

            pe.wait_ge(s_cst, 16)

            def step_a(it, k, r):
                if live(r, 2, NBATCH):
                    b, _, slot = at(it, k, 2)
                    pe.wait_ge(s_uT, b + 1)
                    pe.wait_ge(s_uw, b + 1)
                    if r == 2:
                        pe.wait_ge(s_col, 1)
                    if r >= 4:
                        pe.wait_ge(s_d, b - 1)
                    for j in range(2):
                        dst = bank[2 + 2 * slot + j][:, 0:W1]
                        for c in range(2):
                            T.matmul(dst, uT[:, 2 * slot + c, j * P:(j + 1) * P], wb_s[:, c], start=c == 0, stop=False)
                        for c in range(2):
                            T.matmul(dst, uT[:, 2 * slot + c, j * P + 1:(j + 1) * P + 1], wbf_s[:, c], start=False, stop=False)
                        edge = first1 if j == 0 else last1
                        last = T.matmul(dst, edge, ut[:, 2 * slot + j], start=False, stop=True)
                    last.then_inc(s_P, 1)
                if live(r, 1, NBATCH):
                    b, _, slot = at(it, k, 1)
                    pe.wait_ge(s_u, b + 1)
                    if r >= 3:
                        pe.wait_ge(s_uT, b - 1)
                    transposes(bank[slot], lambda j, c: ut[:, 2 * slot + j, c * P:(c + 1) * P]).then_inc(s_tr, 1)

            steps(pe, step_a, *A_STEPS)
            pe.wait_ge(s_d, NBATCH)
            pe.wait_ge(s_gam, NBATCH)
            pe.wait_ge(s_sq, 2 * NE)
            T.matmul(bank[5][:, 0:2 * NE], const("ones"), sq, start=True, stop=True).then_inc(s_fro, 1)

            def step_b(it, k, r):
                if live(r, 2, NBATCH):
                    b, _, slot = at(it, k, 2)
                    if r == 2:
                        pe.wait_ge(s_scl, 1)
                    pe.wait_ge(s_kr, b + 1)
                    pe.wait_ge(s_qr, b + 1)
                    if r >= 3:
                        pe.wait_ge(s_ret, b)
                    for m in range(2):
                        T.matmul(bank[5][:, 0:SEQ], kr[:, slot, m, 0:P], qr[:, slot, m, :], start=m == 0, stop=m == 1)
                    for m in range(2):
                        last = T.matmul(bank[5][:, SEQ:SEQ + P], kr[:, slot, m, P:SEQ], qr[:, slot, m, P:SEQ],
                                        start=m == 0, stop=m == 1)
                    last.then_inc(s_R, 1)
                if live(r, 4, NBATCH):
                    b, _, _ = at(it, k, 4)
                    pe.wait_ge(s_xnT, b + 1)
                    if r == 4:
                        pe.wait_ge(s_wr, 2)
                    pe.wait_ge(s_sc, b + 1)
                    for j in range(2):
                        for c in range(2):
                            last = T.matmul(bank[7][:, j * NE:(j + 1) * NE], xnT[:, c, j * P:(j + 1) * P], wr_s[:, c],
                                            start=c == 0, stop=c == 1)
                    last.then_inc(s_rtr, 1)
                if live(r, 1, NBATCH):
                    b, half, slot = at(it, k, 1)
                    if r == 1:
                        pe.wait_ge(s_fwb, 64)
                    pe.wait_ge(s_c[slot], 16 * half + 16)
                    if r >= 2:
                        pe.wait_ge(s_rk, b)
                    for m in range(2):
                        for c in range(2):
                            last = T.matmul(bank[2][:, m * SEQ:(m + 1) * SEQ], wk_s[:, c, m * P:(m + 1) * P], cT[:, slot, c],
                                            start=c == 0, stop=c == 1)
                    last.then_inc(s_K, 1)
                    pe.wait_ge(s_u2T, b + 1)
                    if r >= 2:
                        pe.wait_ge(s_rq, b)
                    for m in range(2):
                        for c in range(2):
                            last = T.matmul(bank[3][:, m * SEQ:(m + 1) * SEQ], wq_s[:, c, m * P:(m + 1) * P], u2T[:, c],
                                            start=c == 0, stop=c == 1)
                    last.then_inc(s_Q, 1)
                    if r >= 2:
                        pe.wait_ge(s_vt, b)
                    for j in range(2):
                        for c in range(2):
                            last = T.matmul(bank[4][:, j * D:(j + 1) * D], cT[:, slot, c, j * P:(j + 1) * P], wv_s[:, c],
                                            start=c == 0, stop=c == 1)
                    last.then_inc(s_V, 1)
                if live(r, 0, NBATCH):
                    b, _, _ = at(it, k, 0)
                    pe.wait_ge(s_u2, b + 1)
                    if r >= 1:
                        pe.wait_ge(s_u2T, b)
                    transposes(bank[0], lambda j, c: u2[:, j, c * P:(c + 1) * P]).then_inc(s_tr2, 1)
                if live(r, 2, NBATCH):
                    b, _, slot = at(it, k, 2)
                    pe.wait_ge(s_ret, b + 1)
                    pe.wait_ge(s_vt, b + 1)
                    if r >= 3:
                        pe.wait_ge(s_x2, b)
                    T.matmul(bank[6][:, 0:D], retT[:, 0:P], vt[:, slot, 0], start=True, stop=True)
                    T.matmul(bank[6][:, D:2 * D], retT[:, P:SEQ], vt[:, slot, 0], start=True, stop=False)
                    T.matmul(bank[6][:, D:2 * D], retT[:, SEQ:SEQ + P], vt[:, slot, 1], start=False, stop=True).then_inc(s_O, 1)
                if live(r, 3, NBATCH):
                    b, _, _ = at(it, k, 3)
                    pe.wait_ge(s_xn, b + 1)
                    if r >= 4:
                        pe.wait_ge(s_xnT, b)
                    transposes(bank[1], lambda j, c: xn[:, j, c * P:(c + 1) * P]).then_inc(s_tr3, 1)

            steps(pe, step_b, *B_STEPS)

            pe.wait_ge(s_rd, 12)
            both2 = both.rearrange("p j e -> p (j e)")
            T.matmul(bank[0][:, 0:P], route("before"), both2, start=True, stop=True)
            T.matmul(bank[1][:, 0:P], const("ones"), both2, start=True, stop=True).then_inc(s_cnt, 1)

            pe.wait_ge(s_mark, 1)
            for n in range(2 * NT):
                if n % 8 == 0:
                    pe.wait_ge(s_col32, n // 8 + 1)
                last = T.matmul(bank[2][:, 0:NSLOT], in_col[:, n], marks[:, n], start=n == 0, stop=n == 2 * NT - 1)
            last.then_inc(s_tab, 1)
            pe.wait_ge(s_lo, 2 * NE)
            pe.wait_ge(s_dnw, 16 * NE)
            pe.wait_ge(s_take, 1)

            def step_e(it, k, r):
                if live(r, 2, NSLOT):
                    i, _, _ = at(it, k, 2)
                    pe.wait_ge(s_h, 2 * i + 2)
                    if r >= 3:
                        pe.wait_ge(s_hT, i)
                    for c in range(NH):
                        w = P if c < NH - 1 else HLAST
                        dst = bank[5 + c // 4]
                        last = T.transpose(dst[0:w, (c % 4) * P:(c % 4 + 1) * P], hh[:, c * P:c * P + w], ident)
                    last.then_inc(s_trh, 1)
                if live(r, 0, NSLOT):
                    i, half, slot = at(it, k, 0)
                    pe.wait_ge(s_xs[slot], 16 * half + 16)
                    if r >= 1:
                        pe.wait_ge(s_xsT, i)
                    for n in range(4):
                        last = T.transpose(rowsT_bank[:, n * P:(n + 1) * P], xs[:, slot, n * P:(n + 1) * P], ident16[:, :])
                    last.then_inc(s_trx, 1)
                if live(r, 1, NSLOT):
                    i, _, slot = at(it, k, 1)
                    w0 = pe.snap(pe.value_load(tile_e[0:1, ds(i, 1)], min_val=0, max_val=NE - 1) * (2 * UPC))
                    pe.wait_ge(s_xsT, i + 1)
                    for q in range(4):
                        if r >= 2 and q % 2 == 0:
                            pe.wait_ge(s_h, 2 * i + q // 2 - 1)
                        products = [(c, a, w) for c in range(2) for a, w in ((0, 0), (0, 1), (1, 0))]
                        for n, (c, a, w) in enumerate(products):
                            n0 = c * UPC + w * 2 * H + (1 - q % 2) * H + (q // 2) * HC
                            last = T.matmul(bank[q][:, 0:HC], xsT[:, slot, (2 * a + c) * P:(2 * a + c + 1) * P],
                                            up_w[:, ds(w0 + n0, HC)], start=n == 0, stop=n == len(products) - 1)
                        last.then_inc(s_up, 1)
                if live(r, 2, NSLOT):
                    i, _, _ = at(it, k, 2)
                    w0 = pe.snap(pe.value_load(tile_e[0:1, ds(i, 1)], min_val=0, max_val=NE - 1) * DNC)
                    pe.wait_ge(s_hT, i + 1)
                    if r >= 3:
                        pe.wait_ge(s_yt, i)
                    for c in range(NH):
                        w = P if c < NH - 1 else HLAST
                        last = T.matmul(bank[7][:, 0:D], hT[0:w, c], dn_w[0:w, ds(w0 + c * D, D)], start=c == 0, stop=c == NH - 1)
                    last.then_inc(s_y, 1)

            steps(pe, step_e, *E_STEPS)


def constants():
    import numpy as np
    (at1, n1), (at3, n3), (at2, n2) = const_layout()
    a, d, b = (np.zeros((P, n), np.float32) for n in (n1, n3, n2))

    def put(arr, at, name, v):
        lo, hi = at[name]
        arr[:, lo:hi] = v

    p = np.arange(P)
    put(a, at1, "ident", np.eye(P))
    put(a, at1, "first", (p[:, None] == 0) & (p[None] == 0))
    put(a, at1, "last", (p[:, None] == P - 1) & (p[None] == P - 1))
    u = np.arange(SEQ, dtype=np.float32)
    block = lambda u, v: np.where(u >= v, np.float32(0.96875) ** np.maximum(u - v, 0), 0)
    put(d, at3, "mask", np.concatenate([block(u[None], u[:P, None]), block(u[None, P:], u[P:, None])], 1))
    base = (np.arange(0, D, 2, dtype=np.float32) + np.float32(0.4 * D)) / np.float32(1.4 * D)
    scale = base[:, None] ** (u[None] / np.float32(512.0))
    freq = np.float32(1.0) / np.float32(10000.0) ** (np.arange(P, dtype=np.float32) / np.float32(P))
    angle = freq[:, None] * u[None]
    for n, s in (("q", scale), ("k", 1 / scale)):
        put(d, at3, n + "cos", np.cos(angle) * s)
        put(d, at3, n + "sin", np.concatenate([-np.sin(angle) * s, np.sin(angle) * s], 1))
    put(a, at1, "mhalf", -0.5)
    put(a, at1, "eps", 1e-6)
    put(a, at1, "minus", -1.0)
    put(b, at2, "before", p[:, None] < p[None])
    put(a, at1, "ones", 1.0)
    put(b, at2, "key", np.tile(NE - np.arange(NE), NT)[None])
    put(b, at2, "restart", (np.arange(P) % NT != 0)[None])
    put(b, at2, "steps", np.tile(np.arange(NT) * P, NE)[None])
    put(b, at2, "tileno", np.repeat(np.arange(40), NE)[None])
    put(b, at2, "column", np.arange(P)[None])
    put(b, at2, "tokno", np.tile(np.arange(NT), 2)[None] * P + p[:, None] + 1)
    put(b, at2, "padrow", PADROW + 1 + p[:, None])
    return a, d, b


def kernel(**inputs):
    import numpy as np
    import concourse.bacc as bacc
    from concourse import mybir as mb
    from concourse.bass_utils import run_bass_kernel_spmd as run

    v = {k: np.asarray(a) for k, a in inputs.items()}

    def chunks(w):
        return np.ascontiguousarray(w.reshape(2, P, -1).transpose(1, 0, 2))

    def evens_first(w):
        return w.reshape(D, P, 2).transpose(0, 2, 1).reshape(D, D)

    w_down = np.zeros((NE, NH * P, D), np.float32)
    w_down[:, :H] = v["L0_ffn_w_down"].transpose(0, 2, 1)
    cst, cst_b, cst2 = constants()
    arrays = {
        "x": v["x"],
        "ctxT": np.ascontiguousarray(v["ctx_1024"].transpose(0, 2, 1)),
        "wproj": chunks(v["L0_attn_WB"].T),
        "wproj2": chunks(v["L0_attn_WBf"].T),
        "w1": v["L0_attn_w1"].reshape(D),
        "w2": v["L0_attn_w2"].reshape(D),
        "gbias": v["L0_attn_b"].reshape(1),
        "wq": chunks(evens_first(v["L0_xattn_Wq"].T)),
        "wk": chunks(evens_first(v["L0_xattn_Wk"].T)),
        "wv": chunks(v["L0_xattn_Wv"].T),
        "nscale": np.ascontiguousarray(v["L0_ffn_norm_scale"].reshape(2, P).T),
        "wr": chunks(v["L0_ffn_w_router"].T),
        "wup": np.ascontiguousarray(v["L0_ffn_w_up"].transpose(0, 2, 1).reshape(NE, 2, P, 2 * H)
                                    .transpose(0, 2, 1, 3).reshape(NE, P, UPC)),
        "wdn": np.ascontiguousarray(w_down.reshape(NE, NH, P, D).transpose(0, 2, 1, 3).reshape(NE, P, DNC)),
        "consts": cst,
        "consts_b": cst_b,
        "consts2": cst2,
    }
    nc = bacc.Bacc("TRN2", target_bir_lowering=False, num_devices=1)
    args = [nc.dram_tensor(f"in_{n}", a.shape, mb.dt.float32, kind="ExternalInput").ap() for n, a in arrays.items()]
    xrow_hbm = nc.dram_tensor("xrow_hbm", (NTOK, XROW), mb.dt.float32, kind="Internal").ap()
    out = nc.dram_tensor("out", (NTOK + P, D), mb.dt.float32, kind="ExternalOutput").ap()
    build(nc, *args, xrow_hbm, out)
    r = run(nc, [{f"in_{n}": np.asarray(a, np.float32) for n, a in arrays.items()}], core_ids=[0])
    return r.results[0]["out"][:NTOK].reshape(NBATCH, SEQ, D)
```

```python
import concourse.bass as bass
from concourse import mybir
from contextlib import ExitStack

P = 128
NBATCH = 8
SEQ = 256
D = 256
NT = NBATCH * SEQ // P
NE = 8
H = 704
HA = 512
HB = H - HA
NH = 6
HLAST = H - (NH - 1) * P
UPC = 2 * 2 * H
DNC = NH * D
NSLOT = 2 * NT + NE - 1
W1 = D + 2
NTOK = NT * P
PADROW = NTOK
XROW = D + NE
XSCALE = 1024.0
WSCALE = 16384.0


def const_layout():
    out = []
    for names in ((("ident", P), ("ones", P), ("last", P), ("edge", 2), ("mhalf", NT), ("minus", NT)),
                  (("mask", 384), ("qcos", SEQ), ("qsin", 2 * SEQ), ("kcos", SEQ), ("ksin", 2 * SEQ)),
                  (("before", P), ("key", NT * NE), ("restart", P), ("steps", P), ("tileno", 40 * NE),
                   ("column", P), ("starts", NSLOT), ("tokno", 2 * NT), ("padrow", 1))):
        at, cols = {}, 0
        for name, n in names:
            at[name] = (cols, cols + n)
            cols += n
        out.append((at, cols))
    return out


def build(nc, x, ctxT, wproj, wproj2, w1, w2, gbias, wq, wk, wv, nscale, wr, wup, wdn, consts, consts_b, consts2, xrow_hbm, out):
    fp32, fp16, bf16, i32 = mybir.dt.float32, mybir.dt.float16, mybir.dt.bfloat16, mybir.dt.int32
    ALU, ACT, AX = mybir.AluOpType, mybir.ActivationFunctionType, mybir.AxisListType
    ds = bass.ds
    (at_const, n_const), (at_const_b, n_const_b), (at_route, n_route) = const_layout()
    ctx = ExitStack()
    with ctx:
        def sb(name, shape, dt=fp32):
            return ctx.enter_context(nc.sbuf_tensor(name, shape, dt))

        def sem(name):
            return ctx.enter_context(nc.semaphore(name))

        expert_w = sb("expert_w", [P, NE * (UPC + DNC)])
        up_raw = expert_w[:, UPC:(NE + 1) * UPC]
        up_w = expert_w[:, 0:NE * UPC].bitcast(fp16)
        dn_w = expert_w[:, NE * UPC:NE * (UPC + DNC)]
        assert UPC <= 2 * DNC
        rows = sb("rows", [P, NT, D])
        cst = sb("cst", [P, n_const])
        cst_b = sb("cst_b", [P, n_const_b])
        front = sb("front", [P, 2 * W1 + 3 * 512 + 2 + 2 * NE + 1])
        ident16 = sb("ident16", [P, P], fp16)
        small = sb("small", [P, 64 + 4 * NT + 22 + 88])
        take_idx = sb("take_idx", [P, NSLOT], i32)
        add_idx = sb("add_idx", [P, NSLOT], i32)
        tile_e = sb("tile_e", [1, 40], i32)
        arena = sb("arena", [P, 8104])

        def view(base, lo, *shape):
            n = 1
            for s in shape:
                n *= s
            v = base[:, lo:lo + n]
            if len(shape) == 2:
                v = v.rearrange("p (a b) -> p a b", a=shape[0])
            if len(shape) == 3:
                v = v.rearrange("p (a b c) -> p a b c", a=shape[0], b=shape[1])
            return v

        def const(name):
            if name in at_const:
                lo, hi = at_const[name]
                return cst[:, lo:hi]
            lo, hi = at_const_b[name]
            return cst_b[:, lo:hi]

        ident = const("ident")
        wb_s = view(front, 0, 2, W1)
        o = 2 * W1
        wq_s = view(front, o, 2, D)
        wk_s = view(front, o + 512, 2, D)
        wv_s = view(front, o + 1024, 2, D)
        ns_s = view(front, o + 1536, 2)
        wr_s = view(front, o + 1538, 2, NE)
        gb_s = view(front, o + 1538 + 2 * NE, 1)
        assert n_route <= 1536
        cst2 = view(front, o, n_route)

        def route(name):
            lo, hi = at_route[name]
            return cst2[:, lo:hi]

        st6 = view(small, 0, 4, 6)
        mv1 = view(small, 24, 2, 2, 2)
        ve1 = view(small, 32, 2, 2)
        rstd1 = view(small, 36, 2, 2)
        gam = view(small, 40, 2, 2)
        mv3 = view(small, 48, 2, 2, 2)
        rstd2 = view(small, 64, NT)
        nb2 = view(small, 64 + NT, NT)
        o = 64 + 2 * NT
        nb1 = view(small, o + 6, 2, 2)
        nb3 = view(small, o + 10, 2, 2)
        mv2 = view(small, o + 14, 2, 2)
        ve2, mean2 = view(small, o + 18, NT), view(small, o + 18 + NT, NT)
        o += 18 + 2 * NT + 4
        ve3 = view(small, o, 2, 2, 2)
        r34 = view(small, o + 8, 2, 2, 2)
        o += 16
        edge_logit = view(small, o, 2, 2)
        gate_bias = view(small, o + 4, 2, 2)
        o += 8
        sq = view(small, o, 2 * NE)
        fro = view(small, o + 2 * NE, NE)
        inv_fro = view(small, o + 3 * NE, NE)
        up_scale = view(small, o + 4 * NE, 2 * NE)
        descale = view(small, o + 6 * NE, NE)

        ut = view(arena, 0, 4, W1)
        uT = view(arena, 2056, 4, W1)
        w1_s = view(arena, 3600, D)
        w2_s = view(arena, 3856, D)
        wbf_s = view(arena, 4112, 2, W1)
        w1_edge = view(arena, 5332, D)
        w2_edge = view(arena, 5588, D)
        squares = view(arena, 4112 + 2 * W1, 2 * H // 2).bitcast(bf16)
        o = 6056
        cT = view(arena, o, 2, 2, SEQ)
        u2 = view(arena, o + 1024, 2, D)
        u2T = view(arena, o + 1536, 2, SEQ)
        rot = view(arena, 0, 2, 2, SEQ)
        kr = view(arena, 1024, 2, 2, SEQ)
        qr = view(arena, 2048, 2, 2, SEQ)
        vt = view(arena, 3072, 2, 2, D)
        retT = view(arena, 4096, 384)
        xn = view(arena, 4480, 2, D)
        sk = view(arena, 4992, 2, D)
        xnT = view(arena, 5504, 2, SEQ)
        xrow_f = sb("xrow", [P, 2 * D])
        xrow = xrow_f[:, :].bitcast(fp16).rearrange("p (j n) -> p j n", j=2)
        assert 5504 + 512 <= o and 4112 + 2 * W1 + H <= 5332 and o + 2048 <= 8104
        sc = sb("sc", [P, NT, NE])
        def rt(n):
            return view(arena, 128 * n, NT, NE)
        dsc, key1, s2, key2, ex = (rt(n) for n in range(5))
        hot = view(arena, 128 * 5, 2, P).rearrange("p n (j e) -> p n j e", e=NE)
        both, cum, excl, pos = (view(arena, 128 * n, P) for n in range(7, 11))
        pick = view(arena, 128 * 11, 2 * P)
        vec = 128 * 14
        m1, km1, m2, km2, esum, rsum = (view(arena, vec + NT * n, NT) for n in range(6))
        posf = view(arena, vec + 8 * NT, 2 * NT)
        slot_col, slot_tile = (view(arena, vec + n * NT, NT).bitcast(fp16) for n in (10, 11))
        posi = view(arena, vec + 18 * NT, 2 * NT).bitcast(i32)
        column, starts = view(arena, vec + 12 * NT, 64).bitcast(fp16), view(arena, vec + 16 * NT, 20).bitcast(fp16)[:, 0:NSLOT]
        o = vec + 20 * NT
        ntile, ctile, base = (view(arena, o + NE * n, NE) for n in range(3))
        tilef = view(arena, o + 3 * NE, 40)
        cmpt = view(arena, o + 3 * NE + 40, 40 * NE)
        o += 3 * NE + 40 + 40 * NE
        in_tile = view(arena, o, NT * NSLOT).bitcast(fp16).rearrange("p (a n) -> p a n", n=NSLOT)
        o += NT * NSLOT
        marks = view(arena, o, NT * NSLOT).bitcast(fp16).rearrange("p (a n) -> p a n", n=NSLOT)
        o += NT * NSLOT
        in_col = view(arena, o, NT * P).bitcast(fp16).rearrange("p (a n) -> p a n", n=P)
        empty = view(arena, 0, NSLOT)
        assert o + NT * P <= 8104
        xs_row = view(arena, 0, 2, XROW)
        xs = view(arena, 0, 2 * XROW).bitcast(fp16).rearrange("p (s n) -> p s n", s=2)
        xsT = view(arena, 1120, 2 * 2 * P).bitcast(fp16).rearrange("p (s n) -> p s n", s=2)
        pair_scale = view(arena, 1104, 2)
        gate_scale = view(arena, 1108, 2)
        sg = view(arena, 1728, H)
        hh = view(arena, 2432, H)
        hT = view(arena, 3136, NH, P)
        yt = view(arena, 3904, 2, D)

        bank = [ctx.enter_context(nc.psum_tensor(f"bank{i}", [P, 512], fp32)) for i in range(8)]

        s_cst = sem("constants_loaded")
        s_fw = sem("front_weights_loaded")
        s_fwb, s_cstb = sem("stage_b_weights_loaded"), sem("stage_b_constants_loaded")
        s_upw, s_dnw = [sem("up_weights_loaded_0"), sem("up_weights_loaded_1")], sem("down_weights_loaded")
        s_sq, s_fro, s_scl = sem("squares_summed"), sem("norm_ready"), sem("weight_scale_step")
        s_hi, s_lo = sem("weights_high_ready"), sem("weights_low_ready")
        s_wr = sem("router_weights_scaled")
        s_pad = sem("pad_rows_zeroed")
        s_cst2 = sem("routing_constants_loaded")
        s_row = sem("xn_stored")
        s_nb1, s_nb2 = sem("bias1_ready"), sem("bias2_ready")
        s_zero = sem("zeros_written")
        s_x = [sem(f"x_loaded_{b}") for b in range(NBATCH)]
        s_col = sem("gate_weights_step")
        s_st = sem("sums_ready")
        s_mv = sem("mean_var_ready")
        s_ve, s_rstd = sem("var_eps_ready"), sem("rstd_ready")
        s_u, s_uw, s_gb = sem("u_ready"), sem("edge_logits_ready"), sem("gate_bias_ready")
        s_xu = sem("x_plus_u_ready")
        s_tr, s_uT = sem("u_transposed"), sem("uT_ready")
        s_P, s_gam = sem("projected"), sem("gate_ready")
        s_x1 = sem("x1_ready")
        s_st2, s_mv2, s_ve2, s_rstd2 = sem("sums2_ready"), sem("mean_var2_ready"), sem("var_eps2_ready"), sem("rstd2_ready")
        s_c = [sem("ctx_loaded_0"), sem("ctx_loaded_1")]
        s_u2, s_tr2, s_u2T = sem("u2_ready"), sem("u2_transposed"), sem("u2T_ready")
        s_K, s_Q, s_V = sem("k_ready"), sem("q_ready"), sem("v_ready")
        s_rk, s_rq = sem("k_bank_read"), sem("q_bank_read")
        s_kr, s_qr = sem("k_rotated"), sem("q_rotated")
        s_vt = sem("v_copied")
        s_R, s_ret = sem("scores_ready"), sem("retention_ready")
        s_O, s_x2 = sem("retained_ready"), sem("x2_ready")
        s_st3, s_mv3, s_ve3, s_r34 = sem("sums3_ready"), sem("mean_var3_ready"), sem("var_eps3_ready"), sem("scales3_ready")
        s_pp = sem("pool_step")
        s_s, s_x2s, s_out0 = sem("skip_ready"), sem("x2_plus_skip_ready"), sem("skip_stored")
        s_xh, s_xl, s_xn = sem("xn_high_ready"), sem("xn_low_ready"), sem("xn_ready")
        s_tr3, s_xnT = sem("xn_transposed"), sem("xnT_ready")
        s_rtr, s_sc = sem("router_ready"), sem("router_scores_copied")
        s_rd = sem("routing_step")
        s_ex = sem("exponents_ready")
        s_cnt = sem("counts_ready")
        s_prob, s_te = sem("probabilities_ready"), sem("tile_experts_ready")
        s_probs, s_ps = sem("probabilities_stored"), sem("pair_scale_ready")
        s_gs = sem("gate_scale_ready")
        s_mark, s_col32, s_tab = sem("pair_marks_ready"), sem("pair_columns_ready"), sem("slot_table_summed")
        s_take = sem("slot_table_ready")
        s_xs = [sem("slot_rows_loaded_0"), sem("slot_rows_loaded_1")]
        s_trx, s_xsT = sem("rows_transposed"), sem("rowsT_ready")
        s_up = sem("up_part_ready")
        s_sg, s_h = sem("silu_ready"), sem("h_part_ready")
        s_trh, s_hT = sem("h_transposed"), sem("hT_ready")
        s_y, s_yt = sem("y_ready"), sem("y_copied")
        s_add = sem("y_added")

        spare = sb("spare", [P, 2])
        pad_zero = sb("pad_zero", [P, D])

        rowsT_bank = bank[4][:, 0:2 * P].bitcast(fp16)

        block = ctx.enter_context(nc.Block())

        def at(it, k, d):
            off = k - d
            return (it * 2 + off if off else it * 2), (it + off // 2 if off // 2 else it), off % 2

        def wait_apart(eng, *waits):
            for s, v in waits:
                eng.wait_ge(s, v)
            nc.vector.tensor_copy(spare[:, 0:1], spare[:, 0:1])

        def live(r, d, n):
            return 0 <= r - d < n

        def steps(eng, step, n, lo, hi):
            for t in range(lo):
                step(t // 2, t % 2, t)
            with eng.Fori(lo // 2, hi // 2) as it:
                step(it, 0, lo)
                step(it, 1, lo + 1)
            for t in range(hi, n):
                step(t // 2, t % 2, t)

        def raw_chunk(e, c):
            return up_raw[:, ds(e * UPC + c * 2 * H, 2 * H)]

        def part(e, c, low):
            return up_w[:, ds(e * 2 * UPC + c * UPC + low * 2 * H, 2 * H)]

        def split_chunks(it, k, r):
            if r in (1, 2, 3):
                return [(r - 1, 0), (r - 1, 1)]
            if 4 <= r < NBATCH:
                return [(it + 1, k)]
            return [(r - 3, 0), (r - 3, 1)] if NBATCH <= r < NBATCH + 3 else []

        MARK_LINKS, TILE_LINKS = 16, 30
        A_STEPS = (NBATCH + 3, 4, 8)
        B_STEPS = (NBATCH + 4, 4, 8)
        E_STEPS = (NSLOT + 2, 4, 38)

        @block.sync
        def _(sp):
            def load_x(b):
                sp.dma_start(rows[:, 2 * b:2 * b + 2, :], x[b].rearrange("(j p) n -> p j n", p=P)).then_inc(s_x[b], 16)

            load_x(0)
            sp.dma_start(cst[:, :], consts).then_inc(s_cst, 16)
            for dst, src in ((w1_s, w1.partition_broadcast(P)), (w2_s, w2.partition_broadcast(P)), (wb_s[:, :, 0:D], wproj),
                             (wbf_s[:, :, 0:D], wproj2), (gb_s, gbias.partition_broadcast(P)), (ns_s, nscale)):
                sp.dma_start(dst, src).then_inc(s_fw, 16)
            def load_up(e, k):
                sp.dma_start(up_raw[:, ds(e * UPC, UPC)], wup[ds(e, 1)].rearrange("o p n -> (o p) n")).then_inc(s_upw[k], 16)

            for b in range(1, 4):
                load_x(b)
            load_up(0, 0)
            for b in range(4, NBATCH):
                load_x(b)
            load_up(1, 1)

            def load_ctx(b, slot):
                sp.dma_start(cT[:, slot], ctxT[ds(b, 1)].rearrange("o (c p) n -> p (o c) n", p=P)).then_inc(s_c[slot], 16)

            with sp.Fori(1, NE // 2) as it:
                for k in range(2):
                    sp.wait_ge(s_sq, 4 * it + 2 * k - 2)
                    load_up(it * 2 + k if k else it * 2, k)

            load_ctx(0, 0)
            load_ctx(1, 1)
            for dst, src in ((wk_s, wk), (wq_s, wq), (wv_s, wv), (wr_s, wr)):
                sp.dma_start(dst, src).then_inc(s_fwb, 16)
            sp.dma_start(cst_b[:, :], consts_b).then_inc(s_cstb, 16)

            def step_b(it, k, r):
                if 2 <= r < NBATCH:
                    b, _, slot = at(it, k, 0)
                    sp.wait_ge(s_V, b - 1)
                    load_ctx(b, slot)
                if 2 <= r < NE:
                    e, _, _ = at(it, k, 0)
                    load_down(e)
                if r == NBATCH:
                    sp.wait_ge(s_V, NBATCH)
                    sp.dma_start(cst2, consts2).then_inc(s_cst2, 16)
                if live(r, 3, NBATCH):
                    b, _, _ = at(it, k, 3)
                    sp.wait_ge(s_xl, b + 1)
                    sp.dma_start(xrow_hbm[ds(b * SEQ, SEQ), 0:D].rearrange("(j p) n -> p j n", p=P),
                                 xrow_f[:, :].rearrange("p (j n) -> p j n", j=2)).then_inc(s_row, 16)
                    sp.wait_ge(s_x2s, b + 1)
                    sp.dma_start(out[ds(b * SEQ, SEQ), :].rearrange("(j p) n -> p j n", p=P), rows[:, ds(b * 2, 2), :]).then_inc(s_out0, 16)

            def load_down(e):
                sp.dma_start(dn_w[:, ds(e * DNC, DNC)], wdn[ds(e, 1)].rearrange("o p n -> (o p) n")).then_inc(s_dnw, 16)

            steps(sp, step_b, *B_STEPS)
            for e in range(2):
                sp.wait_ge(s_lo, 2 * NE)
                load_down(e)
            sp.wait_ge(s_prob, 1)
            sp.dma_start(xrow_hbm[:, D:XROW].rearrange("(j p) n -> p j n", p=P), ex).then_inc(s_probs, 16)

        @block.scalar
        def _(act):
            act.wait_ge(s_cst, 16)
            nc.scalar.activation(ident16[:, :], ident, ACT.Copy).then_inc(s_sc, 1)

            def square(it, k, r, c):
                if live(r, 2, NE):
                    e, half, slot = at(it, k, 2)
                    if c == 0:
                        act.wait_ge(s_upw[slot], 16 * half + 16)
                    if r > 2 or c:
                        act.wait_ge(s_sq, 2 * e + c)
                    nc.scalar.activation(squares, raw_chunk(e, c), ACT.Square, scale=ns_s[:, c:c + 1],
                                         accum_out=sq[:, ds(e * 2 + c, 1)]).then_inc(s_sq, 1)

            def step_a(it, k, r):
                if r == 2:
                    act.wait_ge(s_fw, 96)
                if live(r, 1, NBATCH):
                    b, _, slot = at(it, k, 1)
                    act.wait_ge(s_nb1, b + 1)
                    if r >= 3:
                        act.wait_ge(s_P, b - 1)
                        act.wait_ge(s_xu, b - 1)
                        act.wait_ge(s_uw, b - 1)
                    for j in range(2):
                        last = nc.scalar.activation(ut[:, 2 * slot + j, 0:D], rows[:, ds(b * 2 + j, 1), :].squeeze(1), ACT.Identity,
                                                    bias=nb1[:, slot, j:j + 1], scale=rstd1[:, slot, j:j + 1])
                    last.then_inc(s_u, 1)
                square(it, k, r, 0)
                if live(r, 1, NBATCH):
                    b, _, slot = at(it, k, 1)
                    act.wait_ge(s_tr, b + 1)
                    if r < 3:
                        act.wait_ge(s_zero, 1)
                    nc.scalar.activation(uT[:, 2 * slot:2 * slot + 2, 1:SEQ],
                                         bank[slot][:, :].rearrange("p (c n) -> p c n", c=2)[:, :, 1:SEQ],
                                         ACT.Copy).then_inc(s_uT, 1)
                square(it, k, r, 1)
                if live(r, 2, NBATCH):
                    b, _, slot = at(it, k, 2)
                    act.wait_ge(s_gb, b + 1)
                    act.wait_ge(s_P, b + 1)
                    for j in range(2):
                        last = nc.scalar.activation(gam[:, slot, j:j + 1], bank[2 + 2 * slot + j][:, D:D + 1],
                                                    ACT.Sigmoid, bias=gate_bias[:, slot, j:j + 1])
                    last.then_inc(s_gam, 1)

            steps(act, step_a, *A_STEPS)

            def high_parts(chunks):
                for e, c in chunks:
                    if not isinstance(e, int) or e > 0:
                        act.wait_ge(s_lo, e * 2 + c - 1)
                    elif c == 0:
                        act.wait_ge(s_scl, 4)
                    nc.scalar.activation(part(e, c, 0), raw_chunk(e, c), ACT.Copy,
                                         scale=up_scale[:, ds(e * 2 + c, 1)]).then_inc(s_hi, 1)

            def xn_high(b):
                if not isinstance(b, int) or b > 0:
                    act.wait_ge(s_row, 16 * b)
                nc.scalar.activation(xrow[:, :, 0:D], xn, ACT.Copy).then_inc(s_xh, 1)

            def step_b(it, k, r):
                if 4 <= r <= NBATCH:
                    high_parts(split_chunks(it, k, r))
                if live(r, 3, NBATCH):
                    b, _, slot = at(it, k, 3)
                    act.wait_ge(s_r34, b + 1)
                    if r >= 4:
                        act.wait_ge(s_x2s, b)
                    for j in range(2):
                        last = nc.scalar.activation(sk[:, j], rows[:, ds(b * 2 + j, 1), :].squeeze(1), ACT.Identity,
                                                    bias=nb3[:, slot, j:j + 1], scale=r34[:, slot, 0, j:j + 1])
                    last.then_inc(s_s, 1)
                if live(r, 0, NBATCH):
                    b, _, _ = at(it, k, 0)
                    act.wait_ge(s_nb2, b + 1)
                    if r >= 1:
                        act.wait_ge(s_tr2, b)
                    for j in range(2):
                        last = nc.scalar.activation(u2[:, j], rows[:, ds(b * 2 + j, 1), :].squeeze(1), ACT.Identity,
                                                    bias=nb2[:, ds(b * 2 + j, 1)], scale=rstd2[:, ds(b * 2 + j, 1)])
                    last.then_inc(s_u2, 1)
                if live(r, 1, NBATCH):
                    b, _, slot = at(it, k, 1)
                    act.wait_ge(s_V, b + 1)
                    if r == 1:
                        act.wait_ge(s_x1, NBATCH)
                    if r >= 3:
                        act.wait_ge(s_O, b - 1)
                    nc.scalar.activation(vt[:, slot], bank[4][:, :].rearrange("p (c n) -> p c n", c=2),
                                         ACT.Copy).then_inc(s_vt, 1)
                if live(r, 0, NBATCH):
                    b, _, _ = at(it, k, 0)
                    act.wait_ge(s_tr2, b + 1)
                    if r >= 1:
                        act.wait_ge(s_Q, b)
                    nc.scalar.activation(u2T, bank[0][:, :].rearrange("p (c n) -> p c n", c=2),
                                         ACT.Copy).then_inc(s_u2T, 1)
                if r in (2, 3):
                    high_parts(split_chunks(it, k, r))
                if live(r, 3, NBATCH):
                    b, _, _ = at(it, k, 3)
                    if r == NBATCH + 2:
                        high_parts([(NE - 1, 0)])
                    act.wait_ge(s_tr3, b + 1)
                    if r >= 4:
                        act.wait_ge(s_rtr, b)
                    nc.scalar.activation(xnT, bank[1][:, :].rearrange("p (c n) -> p c n", c=2),
                                         ACT.Copy).then_inc(s_xnT, 1)
                    if r < NBATCH + 2:
                        xn_high(b)
                if r == 1:
                    high_parts(split_chunks(it, k, r))
                if r == NBATCH:
                    high_parts([(NE - 2, 0), (NE - 2, 1)])
                if live(r, 4, NBATCH):
                    b, _, _ = at(it, k, 4)
                    act.wait_ge(s_rtr, b + 1)
                    nc.scalar.activation(sc[:, ds(b * 2, 2), :],
                                         bank[7][:, 0:2 * NE].rearrange("p (j e) -> p j e", j=2),
                                         ACT.Copy).then_inc(s_sc, 1)
                    if r == NBATCH + 2:
                        high_parts([(NE - 1, 1)])
                    if r == NBATCH + 3:
                        xn_high(b)

            steps(act, step_b, *B_STEPS)
            act.wait_ge(s_rd, 4)
            nc.scalar.activation(ex, dsc, ACT.Exp).then_inc(s_ex, 1)
            nc.scalar.activation(spare[:, 1:2], const("mhalf")[:, 0:1], ACT.Silu)

            act.wait_ge(s_te, 1)
            act.wait_ge(s_scl, 6)

            def step_e(it, k, r):
                if live(r, 0, NSLOT):
                    i, _, slot = at(it, k, 0)
                    act.wait_ge(s_trx, i + 1)
                    if r >= 2:
                        act.wait_ge(s_up, 3 * i - 3)
                    nc.scalar.activation(xsT[:, slot], rowsT_bank, ACT.Copy).then_inc(s_xsT, 1)
                if live(r, 1, NSLOT):
                    i, _, slot = at(it, k, 1)
                    e = act.snap(act.value_load(tile_e[0:1, ds(i, 1)], min_val=0, max_val=NE - 1))
                    nc.scalar.activation(gate_scale[:, slot:slot + 1], descale[:, ds(e, 1)], ACT.Copy).then_inc(s_gs, 1)
                    act.wait_ge(s_gs, i + 1)
                    for q, (src, cols) in enumerate(((bank[0][:, 0:HA], slice(0, HA)), (bank[2][:, 0:HB], slice(HA, H)))):
                        act.wait_ge(s_up, 3 * i + 2 * q + 1)
                        if r >= 2:
                            act.wait_ge(s_h, 2 * i + q - 1)
                        nc.scalar.activation(sg[:, cols], src, ACT.Silu, scale=gate_scale[:, slot:slot + 1]).then_inc(s_sg, 1)
                if live(r, 2, NSLOT):
                    i, _, slot = at(it, k, 2)
                    act.wait_ge(s_y, i + 1)
                    if r >= 4:
                        act.wait_ge(s_add, 16 * i - 16)
                    nc.scalar.activation(yt[:, slot], bank[7][:, 0:D], ACT.Copy).then_inc(s_yt, 1)

            steps(act, step_e, *E_STEPS)

        @block.gpsimd
        def _(pool):
            pool.memset(uT[:, :, 0:1], 0.0)
            pool.memset(uT[:, :, SEQ:SEQ + 1], 0.0).then_inc(s_zero, 1)
            pool.memset(pad_zero[:, :], 0.0).then_inc(s_zero, 1)
            pool.wait_ge(s_zero, 2)
            pool.dma_start(out[PADROW:PADROW + P, :], pad_zero[:, :]).then_inc(s_pad, 16)
            pool.wait_ge(s_cst, 16)
            mhalf, minus = const("mhalf"), const("minus")

            def step_a(it, k, r):
                if live(r, 0, NBATCH):
                    b, _, slot = at(it, k, 0)
                    pool.wait_ge(s_ve, b + 1)
                    nc.gpsimd.tensor_tensor(rstd1[:, slot], ve1[:, slot], mhalf[:, 0:2], ALU.pow).then_inc(s_rstd, 1)
                    pool.wait_ge(s_rstd, 2 * b + 1)
                    nc.gpsimd.tensor_tensor(nb1[:, slot], mv1[:, slot, :, 0], rstd1[:, slot], ALU.mult).then_inc(s_rstd, 1)
                    pool.wait_ge(s_rstd, 2 * b + 2)
                    if r >= 1:
                        pool.wait_ge(s_u, b)
                    nc.gpsimd.tensor_tensor(nb1[:, slot], nb1[:, slot], minus[:, 0:2], ALU.mult).then_inc(s_nb1, 1)
                if live(r, 1, NBATCH):
                    b, _, slot = at(it, k, 1)
                    if r == NBATCH:
                        pool.wait_ge(s_u, NBATCH)
                    nc.gpsimd.tensor_tensor(rows[:, ds(b * 2, 2), :], rows[:, ds(b * 2, 2), :], ut[:, 2 * slot:2 * slot + 2, 0:D],
                                            ALU.add).then_inc(s_xu, 1)
                if r >= NBATCH:
                    m, lo, hi = r - NBATCH, (0, NT - 4, NT - 2)[r - NBATCH], (NT - 4, NT - 2, NT)[r - NBATCH]
                    pool.wait_ge(s_ve2, hi // 2)
                    nc.gpsimd.tensor_tensor(rstd2[:, lo:hi], ve2[:, lo:hi], mhalf[:, 0:hi - lo], ALU.pow).then_inc(s_rstd2, 1)
                    pool.wait_ge(s_rstd2, 2 * m + 1)
                    nc.gpsimd.tensor_tensor(nb2[:, lo:hi], mean2[:, lo:hi], rstd2[:, lo:hi], ALU.mult).then_inc(s_rstd2, 1)
                    pool.wait_ge(s_rstd2, 2 * m + 2)
                    nc.gpsimd.tensor_tensor(nb2[:, lo:hi], nb2[:, lo:hi], minus[:, 0:hi - lo], ALU.mult).then_inc(s_nb2, (hi - lo) // 2)

            steps(pool, step_a, *A_STEPS)
            pool.wait_ge(s_scl, 2)
            nc.gpsimd.tensor_tensor(inv_fro, fro, mhalf[:, 0:NE], ALU.pow).then_inc(s_scl, 1)

            def step_b(it, k, r):
                if live(r, 1, NBATCH):
                    b, _, slot = at(it, k, 1)
                    for n, (bank_read, rotated, dst) in enumerate(((s_rk, s_kr, kr), (s_rq, s_qr, qr))):
                        pool.wait_ge(bank_read, b + 1)
                        if n and r >= 3:
                            pool.wait_ge(s_xn, b - 1)
                        nc.gpsimd.tensor_tensor(dst[:, slot], dst[:, slot], rot[:, n], ALU.add).then_inc(rotated, 1)
                if live(r, 3, NBATCH):
                    b, _, _ = at(it, k, 3)
                    if r > NBATCH:
                        pool.wait_ge(s_xn, r - 2)
                    nc.gpsimd.tensor_tensor(rows[:, ds(b * 2, 2), :], sk, rows[:, ds(b * 2, 2), :], ALU.add).then_inc(s_x2s, 1)
                    pool.wait_ge(s_xh, b + 1)
                    nc.gpsimd.tensor_tensor(xrow[:, :, D:2 * D], xn, xrow[:, :, 0:D], ALU.subtract).then_inc(s_xl, 1)
                if live(r, 2, NBATCH):
                    b, _, slot = at(it, k, 2)
                    pool.wait_ge(s_ve3, 4 * b + 4)
                    nc.gpsimd.tensor_tensor(r34[:, slot], ve3[:, slot], mhalf[:, 0:4].rearrange("p (a j) -> p a j", a=2),
                                            ALU.pow).then_inc(s_pp, 1)
                    pool.wait_ge(s_pp, 2 * b + 1)
                    nc.gpsimd.tensor_tensor(nb3[:, slot], mv3[:, slot, :, 0], r34[:, slot, 0], ALU.mult).then_inc(s_pp, 1)
                    pool.wait_ge(s_pp, 2 * b + 2)
                    nc.gpsimd.tensor_tensor(nb3[:, slot], nb3[:, slot], minus[:, 0:2], ALU.mult).then_inc(s_r34, 1)

            steps(pool, step_b, *B_STEPS)
            pool.wait_ge(s_rd, TILE_LINKS)
            nc.gpsimd.tensor_tensor(marks, in_tile, route("tokno").unsqueeze(2).broadcast_to([P, 2 * NT, NSLOT]),
                                    ALU.mult).then_inc(s_mark, 1)

            pool.wait_ge(s_out0, 16 * NBATCH)
            pool.wait_ge(s_pad, 16)
            pool.wait_ge(s_row, 16 * NBATCH)
            pool.wait_ge(s_probs, 16)
            pool.wait_ge(s_take, 1)

            def take(i):
                if i >= 2:
                    pool.wait_ge(s_trx, i - 1)
                    pool.wait_ge(s_ps, i - 1)
                pool.indirect_dma_start(out=xs_row[:, i % 2], out_offset=None, in_=xrow_hbm,
                                        in_offset=bass.IndirectOffsetOnAxis(ap=take_idx[:, i:i + 1], axis=0)).then_inc(s_xs[i % 2], 16)

            for i in range(3):
                take(i)
            for i in range(NSLOT):
                if i + 3 < NSLOT:
                    take(i + 3)
                pool.wait_ge(s_yt, i + 1)
                if i:
                    pool.wait_ge(s_add, 16 * i)
                pool.indirect_dma_start(out=out, in_=yt[:, i % 2], in_offset=None,
                                        out_offset=bass.IndirectOffsetOnAxis(ap=add_idx[:, i:i + 1], axis=0),
                                        compute_op=ALU.add).then_inc(s_add, 16)
            pool.wait_ge(s_add, 16 * NSLOT)

        @block.vector
        def _(dve):
            V = nc.vector
            V.memset(spare[:, 0:1], 0.0)
            dve.wait_ge(s_cst, 16)
            V.memset(wb_s[:, :, D + 1], 0.0)
            V.memset(wbf_s[:, :, D + 1], 0.0)
            def step_a(it, k, r):
                if live(r, 0, NBATCH):
                    b, _, slot = at(it, k, 0)
                    if r < 4 or r >= NBATCH:
                        dve.wait_ge(s_x[r], 16)
                    elif r == 4:
                        for later in range(4, NBATCH):
                            dve.wait_ge(s_x[later], 16)
                    for j in range(2):
                        last = V.bn_stats(st6[:, j], rows[:, ds(b * 2 + j, 1), :].squeeze(1))
                    last.then_inc(s_st, 1)
                    wait_apart(dve, (s_st, b + 1))
                    for j in range(2):
                        last = V.bn_aggr(mv1[:, slot, j], st6[:, j])
                    last.then_inc(s_mv, 1)
                    dve.wait_ge(s_mv, b + 1)
                    V.tensor_scalar(ve1[:, slot], mv1[:, slot, :, 1], 1e-5, None, ALU.add).then_inc(s_ve, 1)
                if r == 0:
                    dve.wait_ge(s_fw, 96)
                    for n, (w, ww) in enumerate(((wb_s, w1_s), (wbf_s, w2_s))):
                        for c in range(2):
                            last = V.tensor_tensor_reduce(out=bank[6 + n][:, c * D:(c + 1) * D], in0=w[:, c, 0:D], in1=ww,
                                                          scale=1.0, scalar=0.0, op0=ALU.mult, op1=ALU.add, accum_out=w[:, c, D:D + 1])
                    last.then_inc(s_col, 1)
                    dve.wait_ge(s_col, 1)
                    for c in range(2):
                        diagonal = wb_s[:, c, c * P:(c + 1) * P]
                        V.tensor_tensor(diagonal, diagonal, ident, ALU.subtract).then_inc(s_col, 1)
                    for j, (ww, we) in enumerate(((w1_s, w1_edge), (w2_s, w2_edge))):
                        V.tensor_scalar(we, ww, const("edge")[:, j:j + 1], None, ALU.mult).then_inc(s_col, 1)
                if live(r, 3, NBATCH):
                    b, _, slot = at(it, k, 3)
                    dve.wait_ge(s_gam, b + 1)
                    dve.wait_ge(s_xu, b + 1)
                    for j in range(2):
                        last = V.scalar_tensor_tensor(out=rows[:, ds(b * 2 + j, 1), :].squeeze(1),
                                                      in0=bank[2 + 2 * slot + j][:, 0:D], scalar=gam[:, slot, j:j + 1],
                                                      in1=rows[:, ds(b * 2 + j, 1), :].squeeze(1), op0=ALU.mult, op1=ALU.add)
                    last.then_inc(s_x1, 1)
                    wait_apart(dve, (s_x1, b + 1))
                    for j in range(2):
                        last = V.bn_stats(st6[:, 2 + j], rows[:, ds(b * 2 + j, 1), :].squeeze(1))
                    last.then_inc(s_st2, 1)
                    wait_apart(dve, (s_st2, b + 1))
                    for j in range(2):
                        last = V.bn_aggr(mv2[:, j], st6[:, 2 + j])
                    last.then_inc(s_mv2, 1)
                    dve.wait_ge(s_mv2, b + 1)
                    V.tensor_scalar(mean2[:, ds(b * 2, 2)], mv2[:, :, 0], 0.0, None, ALU.add)
                    V.tensor_scalar(ve2[:, ds(b * 2, 2)], mv2[:, :, 1], 1e-5, None, ALU.add).then_inc(s_ve2, 1)
                if live(r, 1, NBATCH):
                    b, _, slot = at(it, k, 1)
                    if r == 1:
                        dve.wait_ge(s_col, 5)
                    if r >= 3:
                        dve.wait_ge(s_gam, b - 1)
                    dve.wait_ge(s_u, b + 1)
                    for j, ww in enumerate((w1_edge, w2_edge)):
                        last = V.tensor_tensor_reduce(out=bank[6 + j][:, 0:D], in0=ut[:, 2 * slot + j, 0:D], in1=ww, scale=1.0, scalar=0.0,
                                                      op0=ALU.mult, op1=ALU.add, accum_out=edge_logit[:, slot, j:j + 1])
                    last.then_inc(s_uw, 1)
                    dve.wait_ge(s_uw, b + 1)
                    V.tensor_scalar(gate_bias[:, slot], edge_logit[:, slot], gb_s, None, ALU.add).then_inc(s_gb, 1)

            steps(dve, step_a, *A_STEPS)

            dve.wait_ge(s_fro, 1)
            V.tensor_reduce(fro, bank[1][:, 0:2 * NE].rearrange("p (e c) -> p e c", c=2), AX.X, ALU.add).then_inc(s_scl, 1)
            dve.wait_ge(s_scl, 1)
            V.tensor_scalar(fro, fro, 1e-30, None, ALU.max).then_inc(s_scl, 1)
            dve.wait_ge(s_fwb, 64)
            for c in range(2):
                V.tensor_scalar(wr_s[:, c], wr_s[:, c], ns_s[:, c:c + 1], 1.0 / XSCALE, ALU.mult, ALU.mult).then_inc(s_wr, 1)
            dve.wait_ge(s_cstb, 16)

            def low_parts(chunks):
                for e, c in chunks:
                    dve.wait_ge(s_hi, e * 2 + c + 1)
                    V.scalar_tensor_tensor(out=part(e, c, 1), in0=raw_chunk(e, c), scalar=up_scale[:, ds(e * 2 + c, 1)],
                                           in1=part(e, c, 0), op0=ALU.mult, op1=ALU.subtract).then_inc(s_lo, 1)

            def step_b(it, k, r):
                if live(r, 2, NBATCH):
                    b, _, slot = at(it, k, 2)
                    dve.wait_ge(s_R, b + 1)
                    if r >= 3:
                        dve.wait_ge(s_O, b)
                    V.tensor_tensor(retT, bank[5][:, 0:384], const("mask"), ALU.mult).then_inc(s_ret, 1)
                if live(r, 1, NBATCH):
                    b, _, slot = at(it, k, 1)
                    for n, (ready, rotated, read, used, dst, cos, sin) in enumerate((
                            (s_K, s_kr, s_rk, s_R, kr, const("kcos"), const("ksin")),
                            (s_Q, s_qr, s_rq, s_R, qr, const("qcos"), const("qsin")))):
                        src = bank[2 + n][:, :].rearrange("p (m n) -> p m n", m=2)
                        dve.wait_ge(ready, b + 1)
                        if r >= 2:
                            dve.wait_ge(rotated, b)
                        if r >= 3:
                            dve.wait_ge(used, b - 1)
                        V.tensor_tensor(dst[:, slot], src, cos.unsqueeze(1).broadcast_to([P, 2, SEQ]), ALU.mult)
                        for m in range(2):
                            last = V.tensor_tensor(rot[:, n, m], src[:, 1 - m], sin[:, m * SEQ:(m + 1) * SEQ], ALU.mult)
                        last.then_inc(read, 1)
                if r == 1:
                    dve.wait_ge(s_scl, 3)
                    for c in range(2):
                        last = V.tensor_scalar(up_scale.rearrange("p (e c) -> p e c", c=2)[:, :, c], inv_fro, ns_s[:, c:c + 1], WSCALE,
                                               ALU.mult, ALU.mult)
                    last.then_inc(s_scl, 1)
                    V.tensor_scalar(descale, inv_fro, WSCALE * XSCALE, None, ALU.mult).then_inc(s_scl, 1)
                    dve.wait_ge(s_scl, 5)
                    V.reciprocal(descale, descale).then_inc(s_scl, 1)
                if live(r, 3, NBATCH):
                    b, _, slot = at(it, k, 3)
                    dve.wait_ge(s_s, b + 1)
                    if r >= 4:
                        dve.wait_ge(s_tr3, b)
                        dve.wait_ge(s_xl, b)
                    for j in range(2):
                        last = V.tensor_scalar(xn[:, j], sk[:, j], r34[:, slot, 1, j:j + 1], XSCALE, ALU.mult, ALU.mult)
                    last.then_inc(s_xn, 1)
                if r == 1 or 4 <= r <= NBATCH:
                    low_parts(split_chunks(it, k, r))
                if r == NBATCH + 2:
                    low_parts([(NE - 1, 0)])
                if live(r, 2, NBATCH):
                    b, _, slot = at(it, k, 2)
                    dve.wait_ge(s_O, b + 1)
                    V.tensor_tensor(rows[:, ds(b * 2, 2), :], bank[6][:, :].rearrange("p (j n) -> p j n", j=2),
                                    rows[:, ds(b * 2, 2), :], ALU.add).then_inc(s_x2, 1)
                    wait_apart(dve, (s_x2, b + 1))
                    for j in range(2):
                        last = V.bn_stats(st6[:, 2 + j], rows[:, ds(b * 2 + j, 1), :].squeeze(1))
                    last.then_inc(s_st3, 1)
                    wait_apart(dve, (s_st3, b + 1))
                    for j in range(2):
                        last = V.bn_aggr(mv3[:, slot, j], st6[:, 2 + j])
                    last.then_inc(s_mv3, 1)
                    dve.wait_ge(s_mv3, b + 1)
                    V.tensor_scalar(ve3[:, slot, 0], mv3[:, slot, :, 1], 1e-5, None, ALU.add).then_inc(s_ve3, 1)
                    dve.wait_ge(s_ve3, 4 * b + 1)
                    V.reciprocal(ve3[:, slot, 1], ve3[:, slot, 0]).then_inc(s_ve3, 1)
                    dve.wait_ge(s_ve3, 4 * b + 2)
                    V.tensor_tensor(ve3[:, slot, 1], ve3[:, slot, 1], mv3[:, slot, :, 1], ALU.mult).then_inc(s_ve3, 1)
                    dve.wait_ge(s_ve3, 4 * b + 3)
                    V.tensor_scalar(ve3[:, slot, 1], ve3[:, slot, 1], 1e-6, None, ALU.add).then_inc(s_ve3, 1)

                if r in (2, 3, NBATCH + 1):
                    low_parts(split_chunks(it, k, r))

            steps(dve, step_b, *B_STEPS)

            done = [0]

            def link(ins):
                done[0] += 1
                ins.then_inc(s_rd, 1)
                dve.wait_ge(s_rd, done[0])

            def wide(v):
                return v.unsqueeze(2).broadcast_to([P, NT, NE])

            dve.wait_ge(s_cst2, 16)
            dve.wait_ge(s_O, NBATCH)
            link(V.tensor_copy(column, route("column")))
            link(V.tensor_copy(starts, route("starts")))
            key = route("key").rearrange("p (j e) -> p j e", j=NT)
            dve.wait_ge(s_sc, NBATCH + 1)
            link(V.tensor_reduce(m1, sc[:, :, :], AX.X, ALU.max))
            link(V.tensor_tensor(dsc, sc[:, :, :], wide(m1), ALU.subtract))
            link(V.scalar_tensor_tensor(out=key1, in0=dsc, scalar=0.0, in1=key, op0=ALU.is_ge, op1=ALU.mult))
            link(V.tensor_reduce(km1, key1, AX.X, ALU.max))
            link(V.tensor_tensor(hot[:, 0], key1, wide(km1), ALU.is_equal))
            link(V.scalar_tensor_tensor(out=s2, in0=hot[:, 0], scalar=-1e30, in1=dsc, op0=ALU.mult, op1=ALU.add))
            link(V.tensor_reduce(m2, s2, AX.X, ALU.max))
            link(V.tensor_tensor(key2, s2, wide(m2), ALU.is_equal))
            link(V.tensor_tensor(key2, key2, key, ALU.mult))
            link(V.tensor_reduce(km2, key2, AX.X, ALU.max))
            link(V.tensor_tensor(hot[:, 1], key2, wide(km2), ALU.is_equal))
            both_ej, cum_ej, excl_ej = (v.rearrange("p (e j) -> p j e", e=NE) for v in (both, cum, excl))
            link(V.tensor_tensor(both_ej, hot[:, 0], hot[:, 1], ALU.add))
            link(V.tensor_tensor_scan(cum, route("restart"), both, 0.0, ALU.mult, ALU.add))
            link(V.tensor_tensor(excl, cum, both, ALU.subtract))
            assert done[0] == MARK_LINKS, done[0]
            dve.wait_ge(s_ex, 1)
            link(V.tensor_reduce(esum, ex, AX.X, ALU.add))
            link(V.reciprocal(rsum, esum))
            V.tensor_tensor(ex, ex, wide(rsum), ALU.mult).then_inc(s_prob, 1)
            low_parts([(NE - 1, 1)])
            dve.wait_ge(s_cnt, 1)
            link(V.tensor_tensor(pick[:, 0:P].rearrange("p (e j) -> p e j", e=NE),
                                 bank[1][:, 0:NE].unsqueeze(2).broadcast_to([P, NE, NT]),
                                 route("steps").rearrange("p (e j) -> p e j", e=NE), ALU.is_gt))
            link(V.tensor_reduce(ntile, pick[:, 0:P].rearrange("p (e j) -> p e j", e=NE), AX.X, ALU.add))
            link(V.tensor_tensor_scan(ctile, const("ones")[:, 0:NE], ntile, 0.0, ALU.mult, ALU.add))
            link(V.tensor_tensor(base, ctile, ntile, ALU.subtract))
            link(V.scalar_tensor_tensor(out=pos.rearrange("p (j e) -> p j e", j=NT), in0=base.unsqueeze(1).broadcast_to([P, NT, NE]),
                                        scalar=float(P), in1=bank[0][:, 0:P].rearrange("p (e j) -> p j e", e=NE),
                                        op0=ALU.mult, op1=ALU.add))
            link(V.tensor_tensor(pick.rearrange("p (n a) -> p n a", n=2), hot.rearrange("p n j e -> p n (j e)"),
                                 pos.unsqueeze(1).broadcast_to([P, 2, P]), ALU.mult))
            link(V.tensor_reduce(posf, pick.rearrange("p (n e) -> p n e", e=NE), AX.X, ALU.add))
            link(V.tensor_copy(posi, posf))
            link(V.tensor_scalar(posi, posi, P - 1, None, ALU.bitwise_and))
            link(V.tensor_copy(slot_col, posi))
            link(V.tensor_tensor(slot_tile, posf, slot_col, ALU.subtract))
            link(V.tensor_tensor(in_tile, slot_tile.unsqueeze(2).broadcast_to([P, 2 * NT, NSLOT]),
                                 starts.unsqueeze(1).broadcast_to([P, 2 * NT, NSLOT]), ALU.is_equal))
            assert done[0] == TILE_LINKS, done[0]
            dve.wait_ge(s_xl, NBATCH)
            dve.wait_ge(s_rtr, NBATCH)
            for n in range(4):
                part_n = slice(8 * n, 8 * n + 8)
                V.tensor_tensor(in_col[:, part_n], slot_col[:, part_n].unsqueeze(2).broadcast_to([P, 8, P]),
                                column.unsqueeze(1).broadcast_to([P, 8, P]), ALU.is_equal).then_inc(s_col32, 1)
            table = bank[2][:, 0:NSLOT]
            dve.wait_ge(s_tab, 1)
            V.tensor_scalar(take_idx[:, :], table, -1.0, 0.0, ALU.add, ALU.max)
            link(V.tensor_scalar(empty, table, 0.0, route("padrow"), ALU.is_equal, ALU.mult))
            V.scalar_tensor_tensor(out=add_idx[:, :], in0=table, scalar=-1.0, in1=empty,
                                   op0=ALU.add, op1=ALU.add).then_inc(s_take, 1)
            link(V.tensor_tensor(cmpt[0:1].rearrange("p (i e) -> p i e", e=NE),
                                 ctile[0:1].unsqueeze(1).broadcast_to([1, 40, NE]),
                                 route("tileno")[0:1].rearrange("p (i e) -> p i e", e=NE), ALU.is_le))
            link(V.tensor_reduce(tilef[0:1], cmpt[0:1].rearrange("p (i e) -> p i e", e=NE), AX.X, ALU.add))
            V.tensor_scalar(tile_e[:, :], tilef[0:1], float(NE - 1), None, ALU.min).then_inc(s_te, 1)
            dve.wait_ge(s_te, 1)

            def step_e(it, k, r):
                if live(r, 2, NSLOT):
                    i, _, _ = at(it, k, 2)
                    dve.wait_ge(s_trh, i + 1)
                    if r >= 3:
                        dve.wait_ge(s_y, i)
                    V.tensor_copy(hT[:, 0:4], bank[5][:, :].rearrange("p (c n) -> p c n", c=4))
                    V.tensor_copy(hT[:, 4], bank[6][:, 0:P])
                    V.tensor_copy(hT[0:HLAST, 5], bank[6][0:HLAST, P:2 * P]).then_inc(s_hT, 1)
                if live(r, 1, NSLOT):
                    i, half, slot = at(it, k, 1)
                    e = dve.snap(dve.value_load(tile_e[0:1, ds(i, 1)], min_val=0, max_val=NE - 1))
                    dve.wait_ge(s_xs[slot], 16 * half + 16)
                    V.tensor_tensor(pair_scale[:, slot:slot + 1], xs_row[:, slot, ds(e + D, 1)], descale[:, ds(e, 1)],
                                    ALU.mult).then_inc(s_ps, 1)
                    dve.wait_ge(s_ps, i + 1)
                    for q, (src, cols) in enumerate(((bank[1][:, 0:HA], slice(0, HA)), (bank[2][:, HB:2 * HB], slice(HA, H)))):
                        dve.wait_ge(s_sg, 2 * i + q + 1)
                        dve.wait_ge(s_up, 3 * i + q + 2)
                        if r >= 2 and q == 0:
                            dve.wait_ge(s_trh, i)
                        V.scalar_tensor_tensor(out=hh[:, cols], in0=src, scalar=pair_scale[:, slot:slot + 1], in1=sg[:, cols],
                                               op0=ALU.mult, op1=ALU.mult).then_inc(s_h, 1)

            steps(dve, step_e, *E_STEPS)

        @block.tensor
        def _(pe):
            T = nc.tensor

            def transposes(dst, src):
                for c in range(2):
                    for j in range(2):
                        last = T.transpose(dst[:, c * SEQ + j * P:c * SEQ + (j + 1) * P], src(j, c), ident)
                return last

            pe.wait_ge(s_cst, 16)

            def project(slot, j):
                dst = bank[2 + 2 * slot + j][:, 0:W1]
                for c in range(2):
                    T.matmul(dst, uT[:, 2 * slot + c, j * P:(j + 1) * P], wb_s[:, c], start=c == 0, stop=False)
                for c in range(2):
                    last = T.matmul(dst, uT[:, 2 * slot + c, j * P + 1:(j + 1) * P + 1], wbf_s[:, c], start=False,
                                    stop=c == 1 and j == 0)
                if j == 1:
                    last = T.matmul(dst[:, 0:D], const("last"), ut[:, 2 * slot + j, 0:D], start=False, stop=True)
                return last

            def step_a(it, k, r):
                if live(r, 2, NBATCH):
                    b, _, slot = at(it, k, 2)
                    pe.wait_ge(s_uT, b + 1)
                    if r == 2:
                        pe.wait_ge(s_col, 5)
                    if r >= 4:
                        pe.wait_ge(s_x1, b - 1)
                    project(slot, 0)
                if live(r, 1, NBATCH):
                    b, _, slot = at(it, k, 1)
                    pe.wait_ge(s_u, b + 1)
                    if r >= 3:
                        pe.wait_ge(s_uT, b - 1)
                    transposes(bank[slot], lambda j, c: ut[:, 2 * slot + j, c * P:(c + 1) * P]).then_inc(s_tr, 1)
                if live(r, 2, NBATCH):
                    _, _, slot = at(it, k, 2)
                    project(slot, 1).then_inc(s_P, 1)

            steps(pe, step_a, *A_STEPS)
            pe.wait_ge(s_uT, NBATCH)
            pe.wait_ge(s_sq, 2 * NE)
            T.matmul(bank[1][:, 0:2 * NE], const("ones"), sq, start=True, stop=True).then_inc(s_fro, 1)

            def keys(slot):
                for m in range(2):
                    for c in range(2):
                        last = T.matmul(bank[2][:, m * SEQ:(m + 1) * SEQ], wk_s[:, c, m * P:(m + 1) * P], cT[:, slot, c],
                                        start=c == 0, stop=c == 1)
                last.then_inc(s_K, 1)

            def scores(it, k, r):
                b, _, slot = at(it, k, 2)
                pe.wait_ge(s_kr, b + 1)
                pe.wait_ge(s_qr, b + 1)
                if r >= 3:
                    pe.wait_ge(s_ret, b)
                for m in range(2):
                    T.matmul(bank[5][:, 0:SEQ], kr[:, slot, m, 0:P], qr[:, slot, m, :], start=m == 0, stop=m == 1)
                for m in range(2):
                    last = T.matmul(bank[5][:, SEQ:SEQ + P], kr[:, slot, m, P:SEQ], qr[:, slot, m, P:SEQ],
                                    start=m == 0, stop=m == 1)
                last.then_inc(s_R, 1)

            def step_b(it, k, r):
                if live(r, 2, NBATCH) and r > 3:
                    scores(it, k, r)
                if live(r, 4, NBATCH):
                    b, _, _ = at(it, k, 4)
                    pe.wait_ge(s_xnT, b + 1)
                    if r == 4:
                        pe.wait_ge(s_wr, 2)
                    pe.wait_ge(s_sc, b + 1)
                    for j in range(2):
                        for c in range(2):
                            last = T.matmul(bank[7][:, j * NE:(j + 1) * NE], xnT[:, c, j * P:(j + 1) * P], wr_s[:, c],
                                            start=c == 0, stop=c == 1)
                    last.then_inc(s_rtr, 1)
                if r == 0:
                    pe.wait_ge(s_fwb, 64)
                    pe.wait_ge(s_c[0], 16)
                    pe.wait_ge(s_x1, NBATCH - 1)
                    keys(0)
                if live(r, 1, NBATCH):
                    b, half, slot = at(it, k, 1)
                    if r >= 2:
                        pe.wait_ge(s_c[slot], 16 * half + 16)
                        pe.wait_ge(s_rk, b)
                        keys(slot)
                    pe.wait_ge(s_u2T, b + 1)
                    if r >= 2:
                        pe.wait_ge(s_rq, b)
                    for m in range(2):
                        for c in range(2):
                            last = T.matmul(bank[3][:, m * SEQ:(m + 1) * SEQ], wq_s[:, c, m * P:(m + 1) * P], u2T[:, c],
                                            start=c == 0, stop=c == 1)
                    last.then_inc(s_Q, 1)
                    if r >= 2:
                        pe.wait_ge(s_vt, b)
                    else:
                        pe.wait_ge(s_x1, NBATCH)
                    for j in range(2):
                        for c in range(2):
                            last = T.matmul(bank[4][:, j * D:(j + 1) * D], cT[:, slot, c, j * P:(j + 1) * P], wv_s[:, c],
                                            start=c == 0, stop=c == 1)
                    last.then_inc(s_V, 1)
                if r in (2, 3):
                    scores(it, k, r)
                if live(r, 0, NBATCH):
                    b, _, _ = at(it, k, 0)
                    pe.wait_ge(s_u2, b + 1)
                    if r >= 1:
                        pe.wait_ge(s_u2T, b)
                    transposes(bank[0], lambda j, c: u2[:, j, c * P:(c + 1) * P]).then_inc(s_tr2, 1)
                if live(r, 2, NBATCH):
                    b, _, slot = at(it, k, 2)
                    pe.wait_ge(s_ret, b + 1)
                    pe.wait_ge(s_vt, b + 1)
                    if r >= 3:
                        pe.wait_ge(s_x2, b)
                    T.matmul(bank[6][:, 0:D], retT[:, 0:P], vt[:, slot, 0], start=True, stop=True)
                    T.matmul(bank[6][:, D:2 * D], retT[:, P:SEQ], vt[:, slot, 0], start=True, stop=False)
                    T.matmul(bank[6][:, D:2 * D], retT[:, SEQ:SEQ + P], vt[:, slot, 1], start=False, stop=True).then_inc(s_O, 1)
                if live(r, 3, NBATCH):
                    b, _, _ = at(it, k, 3)
                    if r == 3:
                        pe.wait_ge(s_scl, 1)
                    pe.wait_ge(s_xn, b + 1)
                    if r >= 4:
                        pe.wait_ge(s_xnT, b)
                    transposes(bank[1], lambda j, c: xn[:, j, c * P:(c + 1) * P]).then_inc(s_tr3, 1)

            steps(pe, step_b, *B_STEPS)

            pe.wait_ge(s_rd, MARK_LINKS)
            T.matmul(bank[1][:, 0:NE], const("ones"), cum.rearrange("p (e j) -> p e j", e=NE)[:, :, NT - 1], start=True, stop=True)
            T.matmul(bank[0][:, 0:P], route("before"), both, start=True, stop=False)
            T.matmul(bank[0][:, 0:P], const("ones"), excl, start=False, stop=True).then_inc(s_cnt, 1)

            pe.wait_ge(s_mark, 1)
            for n in range(2 * NT):
                if n % 8 == 0:
                    pe.wait_ge(s_col32, n // 8 + 1)
                last = T.matmul(bank[2][:, 0:NSLOT], in_col[:, n], marks[:, n], start=n == 0, stop=n == 2 * NT - 1)
            last.then_inc(s_tab, 1)
            pe.wait_ge(s_lo, 2 * NE)
            pe.wait_ge(s_dnw, 16 * NE)
            pe.wait_ge(s_te, 1)

            def step_e(it, k, r):
                if live(r, 2, NSLOT):
                    i, _, _ = at(it, k, 2)
                    pe.wait_ge(s_h, 2 * i + 2)
                    if r >= 3:
                        pe.wait_ge(s_hT, i)
                    for c in range(NH):
                        w = P if c < NH - 1 else HLAST
                        dst = bank[5 + c // 4]
                        last = T.transpose(dst[0:w, (c % 4) * P:(c % 4 + 1) * P], hh[:, c * P:c * P + w], ident)
                    last.then_inc(s_trh, 1)
                if live(r, 0, NSLOT):
                    i, half, slot = at(it, k, 0)
                    pe.wait_ge(s_xs[slot], 16 * half + 16)
                    if r >= 1:
                        pe.wait_ge(s_xsT, i)
                    for n in range(4):
                        last = T.transpose(rowsT_bank[:, n * P:(n + 1) * P], xs[:, slot, n * P:(n + 1) * P], ident16[:, :])
                    last.then_inc(s_trx, 1)
                if live(r, 1, NSLOT):
                    i, _, slot = at(it, k, 1)
                    w0 = pe.snap(pe.value_load(tile_e[0:1, ds(i, 1)], min_val=0, max_val=NE - 1) * (2 * UPC))
                    pe.wait_ge(s_xsT, i + 1)
                    products = [(c, a, w) for c in range(2) for a, w in ((0, 0), (0, 1), (1, 0))]
                    for q, (lo, n) in enumerate(((0, HA), (HA, HA), (2 * HA, 2 * HB))):
                        if r >= 2 and q != 1:
                            pe.wait_ge(s_h, 2 * i - 1 + q // 2)
                        for m, (c, a, w) in enumerate(products):
                            last = T.matmul(bank[q][:, 0:n], xsT[:, slot, (2 * a + c) * P:(2 * a + c + 1) * P],
                                            up_w[:, ds(w0 + c * UPC + w * 2 * H + lo, n)],
                                            start=m == 0, stop=m == len(products) - 1)
                        last.then_inc(s_up, 1)
                if live(r, 2, NSLOT):
                    i, _, _ = at(it, k, 2)
                    w0 = pe.snap(pe.value_load(tile_e[0:1, ds(i, 1)], min_val=0, max_val=NE - 1) * DNC)
                    pe.wait_ge(s_hT, i + 1)
                    if r >= 3:
                        pe.wait_ge(s_yt, i)
                    for c in range(NH):
                        w = P if c < NH - 1 else HLAST
                        last = T.matmul(bank[7][:, 0:D], hT[0:w, c], dn_w[0:w, ds(w0 + c * D, D)], start=c == 0, stop=c == NH - 1)
                    last.then_inc(s_y, 1)

            steps(pe, step_e, *E_STEPS)


def constants():
    import numpy as np
    (at1, n1), (at3, n3), (at2, n2) = const_layout()
    a, d, b = (np.zeros((P, n), np.float32) for n in (n1, n3, n2))

    def put(arr, at, name, v):
        lo, hi = at[name]
        arr[:, lo:hi] = v

    p = np.arange(P)
    put(a, at1, "ident", np.eye(P))
    edge = np.stack([p == 0, p == P - 1], 1)
    put(a, at1, "edge", edge)
    put(a, at1, "last", (p[:, None] == P - 1) & (p[None] == P - 1))
    u = np.arange(SEQ, dtype=np.float32)
    block = lambda u, v: np.where(u >= v, np.float32(0.96875) ** np.maximum(u - v, 0), 0)
    put(d, at3, "mask", np.concatenate([block(u[None], u[:P, None]), block(u[None, P:], u[P:, None])], 1))
    base = (np.arange(0, D, 2, dtype=np.float32) + np.float32(0.4 * D)) / np.float32(1.4 * D)
    scale = base[:, None] ** (u[None] / np.float32(512.0))
    freq = np.float32(1.0) / np.float32(10000.0) ** (np.arange(P, dtype=np.float32) / np.float32(P))
    angle = freq[:, None] * u[None]
    for n, s in (("q", scale), ("k", 1 / scale)):
        put(d, at3, n + "cos", np.cos(angle) * s)
        put(d, at3, n + "sin", np.concatenate([-np.sin(angle) * s, np.sin(angle) * s], 1))
    put(a, at1, "mhalf", -0.5)
    put(a, at1, "minus", -1.0)
    put(b, at2, "before", p[:, None] < p[None])
    put(a, at1, "ones", 1.0)
    put(b, at2, "key", np.tile(NE - np.arange(NE), NT)[None])
    put(b, at2, "restart", (np.arange(P) % NT != 0)[None])
    put(b, at2, "steps", np.tile(np.arange(NT) * P, NE)[None])
    put(b, at2, "tileno", np.repeat(np.arange(40), NE)[None])
    put(b, at2, "column", np.arange(P)[None])
    put(b, at2, "starts", np.arange(NSLOT)[None] * P)
    put(b, at2, "tokno", np.tile(np.arange(NT), 2)[None] * P + p[:, None] + 1)
    put(b, at2, "padrow", PADROW + 1 + p[:, None])
    return a, d, b


def kernel(**inputs):
    import numpy as np
    import concourse.bacc as bacc
    from concourse import mybir as mb
    from concourse.bass_utils import run_bass_kernel_spmd as run

    v = {k: np.asarray(a) for k, a in inputs.items()}

    def chunks(w):
        return np.ascontiguousarray(w.reshape(2, P, -1).transpose(1, 0, 2))

    def evens_first(w):
        return w.reshape(D, P, 2).transpose(0, 2, 1).reshape(D, D)

    w_down = np.zeros((NE, NH * P, D), np.float32)
    w_down[:, :H] = v["L0_ffn_w_down"].transpose(0, 2, 1)
    cst, cst_b, cst2 = constants()
    value, gate = v["L0_ffn_w_up"][:, :H], v["L0_ffn_w_up"][:, H:]
    w_up = np.concatenate([gate[:, :HA], value[:, :HA], gate[:, HA:], value[:, HA:]], 1)
    arrays = {
        "x": v["x"],
        "ctxT": np.ascontiguousarray(v["ctx_1024"].transpose(0, 2, 1)),
        "wproj": chunks(v["L0_attn_WB"].T),
        "wproj2": chunks(v["L0_attn_WBf"].T),
        "w1": v["L0_attn_w1"].reshape(D),
        "w2": v["L0_attn_w2"].reshape(D),
        "gbias": v["L0_attn_b"].reshape(1),
        "wq": chunks(evens_first(v["L0_xattn_Wq"].T)),
        "wk": chunks(evens_first(v["L0_xattn_Wk"].T)),
        "wv": chunks(v["L0_xattn_Wv"].T),
        "nscale": np.ascontiguousarray(v["L0_ffn_norm_scale"].reshape(2, P).T),
        "wr": chunks(v["L0_ffn_w_router"].T),
        "wup": np.ascontiguousarray(w_up.transpose(0, 2, 1).reshape(NE, 2, P, 2 * H)
                                    .transpose(0, 2, 1, 3).reshape(NE, P, UPC)),
        "wdn": np.ascontiguousarray(w_down.reshape(NE, NH, P, D).transpose(0, 2, 1, 3).reshape(NE, P, DNC)),
        "consts": cst,
        "consts_b": cst_b,
        "consts2": cst2,
    }
    nc = bacc.Bacc("TRN2", target_bir_lowering=False, num_devices=1)
    args = [nc.dram_tensor(f"in_{n}", a.shape, mb.dt.float32, kind="ExternalInput").ap() for n, a in arrays.items()]
    xrow_hbm = nc.dram_tensor("xrow_hbm", (NTOK, XROW), mb.dt.float32, kind="Internal").ap()
    out = nc.dram_tensor("out", (NTOK + P, D), mb.dt.float32, kind="ExternalOutput").ap()
    build(nc, *args, xrow_hbm, out)
    r = run(nc, [{f"in_{n}": np.asarray(a, np.float32) for n, a in arrays.items()}], core_ids=[0])
    return r.results[0]["out"][:NTOK].reshape(NBATCH, SEQ, D)
```
